# Optimizing a Trainium2 kernel written in Bass

```python
import numpy as np
import jax
import jax.numpy as jnp

def _softmax(x, axis=-1):
    return jax.nn.softmax(x, axis=axis)

def _gelu(x):
    return jax.nn.gelu(x, approximate=True)

def _silu(x):
    return jax.nn.silu(x)

def _sigmoid(x):
    return jax.nn.sigmoid(x)

def _layernorm(x, axis=-1, eps=1e-05):
    m = jnp.mean(x, axis=axis, keepdims=True)
    v = jnp.var(x, axis=axis, keepdims=True)
    return (x - m) / jnp.sqrt(v + eps)

def _scatter_add(tgt, idx, src, axis=0):
    return tgt.at[idx].add(src)

def _segment_sum(src, seg, n):
    return jax.ops.segment_sum(src, seg, n)
kernel_name = 'mk_vit_tower_cls_d1_tok_img768_r4_23d01a'

def setup_inputs(seed: int=0):
    np.random.seed(seed)
    _w = jnp.asarray

    def _rec_inputs():
        import jax
        import jax.numpy as jnp
        _rk = jax.random.key(seed)
        x = -0.000348323 + 0.999952 * jax.random.normal(jax.random.fold_in(_rk, 1), (64, 3, 112, 112), jnp.float32)
        cls_tok = 0.02 * jax.random.normal(jax.random.fold_in(_rk, 5), (1, 1, 192), jnp.float32)
        return (x, cls_tok)
    x, cls_tok = _rec_inputs()

    def _L0_tok_setup():
        import jax, jax.numpy as jnp
        import numpy as np
        PATCH = 16
        SHIFT = 1
        EPS = 1e-05

        def _shift_image(x, dy, dx):
            B, C, H, W = x.shape
            padded = jnp.pad(x, ((0, 0), (0, 0), (max(0, dy), max(0, -dy)), (max(0, dx), max(0, -dx))))
            return padded[:, :, max(0, -dy):max(0, -dy) + H, max(0, -dx):max(0, -dx) + W]
        key = jax.random.key(seed)
        k1, k2, k3 = jax.random.split(key, 3)
        B, C, H, Wd = (32, 3, 96, 96)
        dim = 192
        in_dim = 15 * PATCH * PATCH
        x = jax.random.normal(k1, (B, C, H, Wd), dtype=jnp.float32)
        W = jax.random.normal(k2, (in_dim, dim), dtype=jnp.float32) * (1.0 / np.sqrt(in_dim))
        b = jax.random.normal(k3, (dim,), dtype=jnp.float32) * 0.02
        gamma = jnp.ones((dim,), dtype=jnp.float32)
        beta = jnp.zeros((dim,), dtype=jnp.float32)
        return {'x': x, 'W': W, 'b': b, 'gamma': gamma, 'beta': beta}
    _L0_tok_all = _L0_tok_setup()
    _L0_tok_in = {k: v for k, v in _L0_tok_all.items() if k in ('W', 'b', 'gamma', 'beta')}
    del _L0_tok_all

    def _L0_attn_setup():
        import jax, jax.numpy as jnp
        import numpy as np
        B, T, D, H = (4, 1024, 192, 12)
        K, V, LR = (D // 2, D, 16)
        HK, HV = (K // H, V // H)
        EPS = 1e-05
        GATE_LOGIT_NORMALIZER = 16.0
        SCALE = HK ** (-0.5)

        def _gla_forward(x, Wq, Wk, Wv, Wgk1, Wgk2, bgk2, Wg, o_norm_w, Wo):
            b, t, _ = x.shape
            q = (x @ Wq).reshape(b, t, H, HK) * SCALE
            kk = (x @ Wk).reshape(b, t, H, HK)
            v = (x @ Wv).reshape(b, t, H, HV)
            gk = jax.nn.log_sigmoid(x @ Wgk1 @ Wgk2 + bgk2) / GATE_LOGIT_NORMALIZER
            gk = gk.reshape(b, t, H, HK)
            qs, ks, vs, gs = (jnp.moveaxis(a, 1, 0) for a in (q, kk, v, gk))

            def step(S, inp):
                q_t, k_t, v_t, g_t = inp
                S = S * jnp.exp(g_t)[..., None] + k_t[..., None] * v_t[..., None, :]
                o_t = jnp.einsum('bhk,bhkv->bhv', q_t, S)
                return (S, o_t)
            S0 = jnp.zeros((b, H, HK, HV), x.dtype)
            _, o = jax.lax.scan(step, S0, (qs, ks, vs, gs))
            o = jnp.moveaxis(o, 0, 1)
            g = (x @ Wg).reshape(b, t, H, HV)
            rms = o * jax.lax.rsqrt(jnp.mean(o * o, axis=-1, keepdims=True) + EPS) * o_norm_w
            o = rms * (g * jax.nn.sigmoid(g))
            return o.reshape(b, t, V) @ Wo
        key = jax.random.key(seed)
        k = jax.random.split(key, 9)

        def w(kk, shape, fan_in):
            return jax.random.normal(kk, shape, jnp.float32) * fan_in ** (-0.5)
        return {'x': jax.random.normal(k[0], (B, T, D), jnp.float32), 'Wq': w(k[1], (D, K), D), 'Wk': w(k[2], (D, K), D), 'Wv': w(k[3], (D, V), D), 'Wgk1': w(k[4], (D, LR), D), 'Wgk2': w(k[5], (LR, K), LR), 'bgk2': jnp.zeros((K,), jnp.float32), 'Wg': w(k[6], (D, V), D), 'o_norm_w': jnp.ones((HV,), jnp.float32), 'Wo': w(k[7], (V, D), V)}
    _L0_attn_all = _L0_attn_setup()
    _L0_attn_in = {k: v for k, v in _L0_attn_all.items() if k in ('Wq', 'Wk', 'Wv', 'Wgk1', 'Wgk2', 'bgk2', 'Wg', 'o_norm_w', 'Wo')}
    del _L0_attn_all

    def _L0_ffn_setup():
        import jax, jax.numpy as jnp
        import numpy as np
        B, S, D = (2, 256, 192)
        NF, NR, R, DS, K = (128, 128, 128, 64, 4)

        @jax.checkpoint
        def feature_fn(x, neurons, weights):
            all_h = jnp.einsum('bsd,ndr->bsnr', x, neurons)
            return jnp.einsum('bsnr,bsn->bsr', all_h, weights)

        @jax.checkpoint
        def restore_fn(h, neurons, weights):
            all_out = jnp.einsum('bsr,nrd->bsnd', h, neurons)
            return jnp.einsum('bsnd,bsn->bsd', all_out, weights)

        def topk_sparsify(weights, k):
            topk_vals, topk_idx = jax.lax.top_k(weights, k)
            N = weights.shape[-1]
            one_hot_mask = jax.nn.one_hot(topk_idx, N, dtype=weights.dtype)
            sparse = (one_hot_mask * topk_vals[..., jnp.newaxis]).sum(axis=-2)
            sparse = sparse / (sparse.sum(axis=-1, keepdims=True) + 1e-08)
            return (sparse, topk_idx)
        key = jax.random.key(seed)
        ks = jax.random.split(key, 8)
        x = jax.random.normal(ks[0], (B, S, D), jnp.float32)
        f_know = jax.random.normal(ks[1], (NF, D, R), jnp.float32) * 0.02
        r_know = jax.random.normal(ks[2], (NR, R, D), jnp.float32) * 0.02
        W_fk = jax.random.normal(ks[3], (D, DS), jnp.float32) * 0.02
        b_fk = jnp.zeros((DS,), jnp.float32)
        W_rk = jax.random.normal(ks[4], (D, DS), jnp.float32) * 0.02
        b_rk = jnp.zeros((DS,), jnp.float32)
        emb_fk = jax.random.normal(ks[5], (NF, DS), jnp.float32) * 0.02
        emb_rk = jax.random.normal(ks[6], (NR, DS), jnp.float32) * 0.02
        return {'x': x, 'f_know': f_know, 'r_know': r_know, 'W_fk': W_fk, 'b_fk': b_fk, 'W_rk': W_rk, 'b_rk': b_rk, 'emb_fk': emb_fk, 'emb_rk': emb_rk}
    _L0_ffn_all = _L0_ffn_setup()
    _L0_ffn_in = {k: v for k, v in _L0_ffn_all.items() if k in ('f_know', 'r_know', 'W_fk', 'b_fk', 'W_rk', 'b_rk', 'emb_fk', 'emb_rk')}
    del _L0_ffn_all
    return {'x': x, 'cls_tok': cls_tok, 'L0_tok_W': _L0_tok_in['W'], 'L0_tok_b': _L0_tok_in['b'], 'L0_tok_gamma': _L0_tok_in['gamma'], 'L0_tok_beta': _L0_tok_in['beta'], 'L0_attn_Wq': _L0_attn_in['Wq'], 'L0_attn_Wk': _L0_attn_in['Wk'], 'L0_attn_Wv': _L0_attn_in['Wv'], 'L0_attn_Wgk1': _L0_attn_in['Wgk1'], 'L0_attn_Wgk2': _L0_attn_in['Wgk2'], 'L0_attn_bgk2': _L0_attn_in['bgk2'], 'L0_attn_Wg': _L0_attn_in['Wg'], 'L0_attn_o_norm_w': _L0_attn_in['o_norm_w'], 'L0_attn_Wo': _L0_attn_in['Wo'], 'L0_ffn_f_know': _L0_ffn_in['f_know'], 'L0_ffn_r_know': _L0_ffn_in['r_know'], 'L0_ffn_W_fk': _L0_ffn_in['W_fk'], 'L0_ffn_b_fk': _L0_ffn_in['b_fk'], 'L0_ffn_W_rk': _L0_ffn_in['W_rk'], 'L0_ffn_b_rk': _L0_ffn_in['b_rk'], 'L0_ffn_emb_fk': _L0_ffn_in['emb_fk'], 'L0_ffn_emb_rk': _L0_ffn_in['emb_rk']}

def reference(x, cls_tok, L0_tok_W, L0_tok_b, L0_tok_gamma, L0_tok_beta, L0_attn_Wq, L0_attn_Wk, L0_attn_Wv, L0_attn_Wgk1, L0_attn_Wgk2, L0_attn_bgk2, L0_attn_Wg, L0_attn_o_norm_w, L0_attn_Wo, L0_ffn_f_know, L0_ffn_r_know, L0_ffn_W_fk, L0_ffn_b_fk, L0_ffn_W_rk, L0_ffn_b_rk, L0_ffn_emb_fk, L0_ffn_emb_rk):
    import jax
    import jax.numpy as jnp

    def _L0_tok_ref(x, W, b, gamma, beta):
        import jax, jax.numpy as jnp
        import numpy as np
        PATCH = 16
        SHIFT = 1
        EPS = 1e-05

        def _shift_image(x, dy, dx):
            B, C, H, W = x.shape
            padded = jnp.pad(x, ((0, 0), (0, 0), (max(0, dy), max(0, -dy)), (max(0, dx), max(0, -dx))))
            return padded[:, :, max(0, -dy):max(0, -dy) + H, max(0, -dx):max(0, -dx) + W]
        s = SHIFT
        x_cat = jnp.concatenate([x, _shift_image(x, -s, -s), _shift_image(x, -s, +s), _shift_image(x, +s, -s), _shift_image(x, +s, +s)], axis=1)
        B, C, H, Wd = x_cat.shape
        P = PATCH
        nh, nw = (H // P, Wd // P)
        patches = x_cat.reshape(B, C, nh, P, nw, P)
        patches = patches.transpose(0, 2, 4, 1, 3, 5)
        patches = patches.reshape(B, nh * nw, C * P * P)
        out = jnp.einsum('bnd,de->bne', patches, W) + b
        mu = jnp.mean(out, axis=-1, keepdims=True)
        var = jnp.mean(jnp.square(out - mu), axis=-1, keepdims=True)
        out = (out - mu) * jax.lax.rsqrt(var + EPS) * gamma + beta
        return out

    def _L0_attn_ref(x, Wq, Wk, Wv, Wgk1, Wgk2, bgk2, Wg, o_norm_w, Wo):
        import jax, jax.numpy as jnp
        import numpy as np
        B, T, D, H = (4, 1024, 192, 12)
        K, V, LR = (D // 2, D, 16)
        HK, HV = (K // H, V // H)
        EPS = 1e-05
        GATE_LOGIT_NORMALIZER = 16.0
        SCALE = HK ** (-0.5)

        def _gla_forward(x, Wq, Wk, Wv, Wgk1, Wgk2, bgk2, Wg, o_norm_w, Wo):
            b, t, _ = x.shape
            q = (x @ Wq).reshape(b, t, H, HK) * SCALE
            kk = (x @ Wk).reshape(b, t, H, HK)
            v = (x @ Wv).reshape(b, t, H, HV)
            gk = jax.nn.log_sigmoid(x @ Wgk1 @ Wgk2 + bgk2) / GATE_LOGIT_NORMALIZER
            gk = gk.reshape(b, t, H, HK)
            qs, ks, vs, gs = (jnp.moveaxis(a, 1, 0) for a in (q, kk, v, gk))

            def step(S, inp):
                q_t, k_t, v_t, g_t = inp
                S = S * jnp.exp(g_t)[..., None] + k_t[..., None] * v_t[..., None, :]
                o_t = jnp.einsum('bhk,bhkv->bhv', q_t, S)
                return (S, o_t)
            S0 = jnp.zeros((b, H, HK, HV), x.dtype)
            _, o = jax.lax.scan(step, S0, (qs, ks, vs, gs))
            o = jnp.moveaxis(o, 0, 1)
            g = (x @ Wg).reshape(b, t, H, HV)
            rms = o * jax.lax.rsqrt(jnp.mean(o * o, axis=-1, keepdims=True) + EPS) * o_norm_w
            o = rms * (g * jax.nn.sigmoid(g))
            return o.reshape(b, t, V) @ Wo
        return _gla_forward(x, Wq, Wk, Wv, Wgk1, Wgk2, bgk2, Wg, o_norm_w, Wo)

    def _L0_ffn_ref(x, f_know, r_know, W_fk, b_fk, W_rk, b_rk, emb_fk, emb_rk):
        import jax, jax.numpy as jnp
        import numpy as np
        B, S, D = (2, 256, 192)
        NF, NR, R, DS, K = (128, 128, 128, 64, 4)

        @jax.checkpoint
        def feature_fn(x, neurons, weights):
            all_h = jnp.einsum('bsd,ndr->bsnr', x, neurons)
            return jnp.einsum('bsnr,bsn->bsr', all_h, weights)

        @jax.checkpoint
        def restore_fn(h, neurons, weights):
            all_out = jnp.einsum('bsr,nrd->bsnd', h, neurons)
            return jnp.einsum('bsnd,bsn->bsd', all_out, weights)

        def topk_sparsify(weights, k):
            topk_vals, topk_idx = jax.lax.top_k(weights, k)
            N = weights.shape[-1]
            one_hot_mask = jax.nn.one_hot(topk_idx, N, dtype=weights.dtype)
            sparse = (one_hot_mask * topk_vals[..., jnp.newaxis]).sum(axis=-2)
            sparse = sparse / (sparse.sum(axis=-1, keepdims=True) + 1e-08)
            return (sparse, topk_idx)
        emb_fk_n = emb_fk / (jnp.linalg.norm(emb_fk, axis=-1, keepdims=True) + 1e-08)
        emb_rk_n = emb_rk / (jnp.linalg.norm(emb_rk, axis=-1, keepdims=True) + 1e-08)
        logits_fk = jnp.einsum('bsd,nd->bsn', x @ W_fk + b_fk, emb_fk_n)
        logits_rk = jnp.einsum('bsd,nd->bsn', x @ W_rk + b_rk, emb_rk_n)
        w_fk, _ = topk_sparsify(jax.nn.softmax(logits_fk, axis=-1), K)
        w_rk, _ = topk_sparsify(jax.nn.softmax(logits_rk, axis=-1), K)
        h = feature_fn(x, f_know, w_fk)
        out = restore_fn(h, r_know, w_rk)
        return out
    h = _L0_tok_ref(x, L0_tok_W, L0_tok_b, L0_tok_gamma, L0_tok_beta)
    h = jnp.concatenate([jnp.broadcast_to(cls_tok, (h.shape[0], 1, h.shape[2])), h], axis=1)
    h = h + _L0_attn_ref(_layernorm(h, axis=-1), L0_attn_Wq, L0_attn_Wk, L0_attn_Wv, L0_attn_Wgk1, L0_attn_Wgk2, L0_attn_bgk2, L0_attn_Wg, L0_attn_o_norm_w, L0_attn_Wo)
    h = h + _L0_ffn_ref(_layernorm(h, axis=-1), L0_ffn_f_know, L0_ffn_r_know, L0_ffn_W_fk, L0_ffn_b_fk, L0_ffn_W_rk, L0_ffn_b_rk, L0_ffn_emb_fk, L0_ffn_emb_rk)
    return h

_drawn_inputs = setup_inputs


def setup_inputs(seed=0):
    import zlib

    import numpy as np

    out = dict(_drawn_inputs(seed))
    spreads = {'L0_tok_gamma': (1.0, 0.2),
     'L0_tok_beta': (0.0, 0.1),
     'L0_attn_bgk2': (0.0, 0.51),
     'L0_attn_o_norm_w': (1.0, 0.2),
     'L0_ffn_b_fk': (0.0, 0.795),
     'L0_ffn_b_rk': (0.0, 0.792)}
    factors = {'L0_ffn_f_know': 4.374,
     'L0_ffn_r_know': 4.387,
     'L0_ffn_W_fk': 4.465,
     'L0_ffn_W_rk': 4.51,
     'L0_ffn_emb_fk': 4.434,
     'L0_ffn_emb_rk': 4.449}
    for name, (base, spread) in spreads.items():
        noise = np.random.default_rng([zlib.crc32(name.encode()), seed]).standard_normal(out[name].shape)
        drawn = base * np.exp(spread * noise) if base else spread * noise
        out[name] = jnp.asarray(drawn.astype(out[name].dtype))
    for name, factor in factors.items():
        out[name] = (out[name] * factor).astype(out[name].dtype)
    return out
```

```python
from contextlib import ExitStack

import numpy as np
import concourse.bass as bass
from concourse import mybir
from concourse.alu_op_type import AluOpType as ALU

ACT = mybir.ActivationFunctionType
F32, BF16 = mybir.dt.float32, mybir.dt.bfloat16
I32, U32, U16 = mybir.dt.int32, mybir.dt.uint32, mybir.dt.uint16
AX = mybir.AxisListType

B, C, HW, PATCH = 64, 3, 112, 16
GRID = HW // PATCH
NPATCH = GRID * GRID
T = NPATCH + 1
D, KD, H = 192, 96, 12
HK, HV = KD // H, D // H
LR = 16
DH = D // 2
PAIRS = B // 2
ROWS = 2 * T
PROWS = 2 * NPATCH
WIN = PATCH + 2
HALF = WIN // 2
KC = C * WIN
XW = HW + 2
EPS = 1e-5
GATE_DIV = 16.0
CLAMP = 43.0 * GATE_DIV

NTOK = B * T
NTILE = NTOK // 128
NN, R, DS, TOPK = 128, 128, 64, 4
GQ = 4
MAXT = (NTOK * TOPK + NN * 127) // 128
NG = -(-MAXT // GQ)
NG += NG % 2
SLOTS = NG * GQ * 128
SH = ((1, 1), (2, 2), (2, 0), (0, 2), (0, 0))


def vit_kernel(nc, x, cls_tok, tok_W, tok_b, tok_gamma, tok_beta, Wq, Wk, Wv, Wgk1, Wgk2, bgk2, Wg,
               o_norm_w, Wo, f_know, r_know, W_fk, b_fk, W_rk, b_rk, emb_fk, emb_rk, out):
    h1_d = nc.dram_tensor("h1_d", [NTOK, D], F32, kind="Internal").ap()
    xs_d = nc.dram_tensor("xs_d", [SLOTS, D], F32, kind="Internal").ap()
    hp_d = nc.dram_tensor("hp_d", [SLOTS, R], F32, kind="Internal").ap()
    hs_d = nc.dram_tensor("hs_d", [SLOTS, R], F32, kind="Internal").ap()
    op_d = nc.dram_tensor("op_d", [SLOTS, D], F32, kind="Internal").ap()
    out_d = out.rearrange("b t d -> (b t) d")

    with ExitStack() as top:
        def sbt(name, shape, dt=F32):
            return top.enter_context(nc.sbuf_tensor(name, shape, dt))

        know = sbt("know", [128, NN * 2 * R])
        ident = sbt("ident", [128, 128])
        mhalf = sbt("mhalf", [128, 32])
        psum = [top.enter_context(nc.psum_tensor(f"bank{i}", [128, 512], F32)) for i in range(8)]
        sems = {}

        def S(name):
            if name not in sems:
                sems[name] = top.enter_context(nc.semaphore(name))
            return sems[name]

        def hold(eng, name, value, who):
            eng.wait_ge(S(name), value)
            eng.sem_inc(S(f"passed_{who}"), 1)

        K = dict(nc=nc, S=S, hold=hold, know=know, ident=ident, mhalf=mhalf, psum=psum, h1_d=h1_d, xs_d=xs_d,
                 hp_d=hp_d, hs_d=hs_d, op_d=op_d, out_d=out_d)
        part1(K, x, cls_tok, tok_W, tok_b, tok_gamma, tok_beta, Wq, Wk, Wv, Wgk1, Wgk2, bgk2, Wg, o_norm_w, Wo,
              f_know)
        part2(K, f_know, r_know, W_fk, b_fk, W_rk, b_rk, emb_fk, emb_rk)


NCHUNK = (PAIRS - 2) // 2
KCH = 6
NMASK = 9
TAIL = NCHUNK * KCH


def part1(K, x, cls_tok, tok_W, tok_b, tok_gamma, tok_beta, Wq, Wk, Wv, Wgk1, Wgk2, bgk2, Wg, o_norm_w, Wo,
          f_know):
    nc, know, ident, mhalf, psum = (K[k] for k in ("nc", "know", "ident", "mhalf", "psum"))
    h1_d, xs_d, hs_d = K["h1_d"], K["xs_d"], K["hs_d"]
    with ExitStack() as ctx:
        def sb(name, shape, dt=F32):
            return ctx.enter_context(nc.sbuf_tensor(name, shape, dt))

        S, hold = K["S"], K["hold"]
        tail0 = TAIL * 2 * R
        h_res = know[:, tail0:tail0 + PAIRS * D].rearrange("p (i d) -> p i d", d=D)
        stage = know[:, 0:5 * HALF * D].rearrange("p (s v e) -> p s v e", s=5, v=HALF)
        zeros = sb("zeros", [128, 512])
        weff = sb("weff", [2 * KC, HALF, D])
        raw = sb("raw", [KC, 2, GRID, XW])
        img = sb("img", [2 * KC, 2, 2, GRID, HW])
        wq = sb("wq", [DH, 2, KD]); wk = sb("wk", [DH, 2, KD])
        wgk = sb("wgk", [DH, 2, KD]); wgk1T = sb("wgk1T", [LR, 2, DH])
        wgk1 = sb("wgk1", [DH, 2, LR]); wgk2 = sb("wgk2", [LR, KD])
        wv = sb("wv", [DH, 2, D]); wg = sb("wg", [DH, 2, D]); wo = sb("wo", [DH, 2, D])
        onw = sb("onw", [DH, 1]); bgk = sb("bgk", [KD, 1])
        tokb = sb("tokb", [128, D]); gam = sb("gam", [128, D]); bet = sb("bet", [128, D])
        causal = sb("causal", [128, T])
        headm = sb("headm", [KD, H])
        carry = sb("carry", [KD, 2, T])
        s0 = sb("s0", [128, D]); st6 = sb("st6", [128, 2, 6]); mv = sb("mv", [128, 2, 2])
        rs0 = sb("rs0", [128, 1]); rs1 = sb("rs1", [128, 1]); ve = sb("ve", [128, 2])
        xn0 = sb("xn0", [128, D]); xg = sb("xg", [128, D]); xn = sb("xn", [ROWS, D])
        hnT = sb("hnT", [DH, 2, 128])
        zz = sb("zz", [KD, ROWS]); mz = sb("mz", [KD, ROWS]); az = sb("az", [KD, ROWS]); ez = sb("ez", [KD, ROWS])
        lz = sb("lz", [KD, ROWS]); gl = sb("gl", [KD, 2, T]); gs = sb("gs", [KD, 2, T])
        dd = sb("dd", [KD, 2, T]); dc = sb("dc", [KD, 2, T]); eq = sb("eq", [KD, ROWS]); ek = sb("ek", [KD, ROWS])
        qt = sb("qt", [KD, 2, T]); kt = sb("kt", [KD, 2, 2, 64]); qx = sb("qx", [KD, 2, 2, H, T])
        vv = sb("vv", [128, 2, H, 2, HV]); att = sb("att", [128, 2, H, T])
        sq = sb("sq", [T, H * 2 * HV]); ms = sb("ms", [T, H * 2]); mse = sb("mse", [T, H * 2]); rso = sb("rso", [T, H * 2])
        on = sb("on", [T, 2, D]); eg = sb("eg", [DH, 2 * ROWS]); eg1 = sb("eg1", [DH, 2 * ROWS])
        sg = sb("sg", [DH, 2 * ROWS]); gate = sb("gate", [DH, 2, 2, ROWS]); oT = sb("oT", [DH, 2, 2, ROWS])

        ps_tok, ps_T, ps_qkg, ps_vg, ps_sa, ps_sb, ps_o, ps_wo = psum
        block = ctx.enter_context(nc.Block())

        N, DEPTH = PAIRS, 3
        T0 = 6

        def ticks(eng, body):
            for t in range(T0):
                body(t, t % 2, lambda d, t=t: 0 <= t - d < N, t)
            with eng.Fori(0, (N - T0) // 2) as j:
                for u in range(2):
                    body(T0 + u + 2 * j, u, lambda d: True, T0)
            for t in range(N, N + DEPTH):
                body(t, t % 2, lambda d, t=t: 0 <= t - d < N, t)

        @block.sync
        def _(eng):
            eng.wait_ge(S("cleared"), 1)
            n = 0
            for s, (u0, v0) in enumerate(SH):
                for c in range(C):
                    wsrc = tok_W[(s * C + c) * PATCH * PATCH:(s * C + c + 1) * PATCH * PATCH, :].rearrange(
                        "(i j) e -> i j e", j=PATCH)
                    nlo = HALF - v0
                    p = c * WIN + u0
                    eng.dma_start(stage[p:p + PATCH, s, v0:HALF, :], wsrc[:, 0:nlo, :]).then_inc(S("w_in"), 16)
                    eng.dma_start(stage[KC + p:KC + p + PATCH, s, 0:PATCH - nlo, :],
                                  wsrc[:, nlo:PATCH, :]).then_inc(S("w_in"), 16)
                    n += 2
            assert n == 30

            xr = x.rearrange("b c (y u) w -> c u b y w", u=PATCH)

            def load_pair(i, u, first):
                if not first or i:
                    hold(eng, "img", i * 32, "sp")
                for b in range(2):
                    src = xr[:, :, bass.ds(i * 2 + b, 1), :, :]
                    for c in range(C):
                        p = c * WIN
                        eng.dma_start(raw[p + 1:p + 17, b, :, 1:1 + HW], src[c, :, 0]).then_inc(S("rows"), 16)
                    eng.dma_start(raw[0:KC:WIN, b, 1:GRID, 1:1 + HW],
                                  src[:, PATCH - 1, 0, 0:GRID - 1, :]).then_inc(S("rows"), 16)
                    eng.dma_start(raw[WIN - 1:KC:WIN, b, 0:GRID - 1, 1:1 + HW],
                                  src[:, 0, 0, 1:GRID, :]).then_inc(S("rows"), 16)
                hold(eng, "rows", i * 160 + 160, "sp")
                if not first:
                    hold(eng, "tok", i - 1, "sp")
                for half in range(2):
                    n = HW if half == 0 else XW - HALF
                    eng.dma_start(img[half * KC:(half + 1) * KC, u, :, :, 0:n],
                                  raw[:, :, :, half * HALF:half * HALF + n]).then_inc(S("img"), 16)

            eng.wait_ge(S("img_clear"), 2)
            load_pair(0, 0, True)
            load_pair(1, 1, True)
            eng.wait_ge(S("weff_done"), 1)
            eng.wait_ge(S("cst"), 9)
            pads = []
            for dst in (xs_d, hs_d):
                flat = dst.rearrange("(p r) d -> p (r d)", p=128)
                total = flat.shape[1]
                pads.append((flat, total, total // NCHUNK // 8 * 8))

            def clear(flat, at, n, m):
                eng.dma_start(flat[:, bass.ds(at, n * m)].rearrange("p (n m) -> p n m", n=n),
                              zeros[:, 0:m].unsqueeze(1).to_broadcast([128, n, m])).then_inc(S("zeroed"), 16)

            with eng.Fori(0, NCHUNK) as j:
                for u in range(2):
                    load_pair(2 * j + 2 + u, u, False)
                for half in range(2):
                    eng.dma_start(know[0:DH, bass.ds(j * (KCH * 2 * R), KCH * 2 * R)].rearrange(
                                      "p (n k r) -> p n k r", k=2, r=R)[:, :, half, :],
                                  f_know[bass.ds(j * KCH, KCH), half * DH:(half + 1) * DH, :].rearrange("n p r -> p n r")
                                  ).then_inc(S("know_in"), 16)
                for flat, total, per in pads:
                    clear(flat, j * per, 8, per // 8)
            for flat, total, per in pads:
                clear(flat, NCHUNK * per, 1, total - NCHUNK * per)
            eng.wait_ge(S("h1"), N)
            h1v = h1_d.rearrange("(i b t) d -> b t i d", b=2, t=T)
            for b in range(2):
                eng.dma_start(h1v[b, 1:T], h_res[b * NPATCH:(b + 1) * NPATCH, :, :]).then_inc(S("h1_out"), 16)
                eng.dma_start(h1v[b, 0:1], h_res[PROWS + b:PROWS + b + 1, :, :]).then_inc(S("h1_out"), 16)
            eng.wait_ge(S("h1_out"), 64)
            eng.wait_ge(S("know_in"), 32 * NCHUNK)
            eng.wait_ge(S("zeroed"), 32 * NCHUNK + 32)

        @block.gpsimd
        def _(eng):
            eng.memset(know[:, 0:5 * HALF * D], 0.0).then_inc(S("cleared"), 1)
            eng.memset(raw[:, :, :, :], 0.0).then_inc(S("img_clear"), 1)
            eng.memset(img[:, :, :, :, :], 0.0).then_inc(S("img_clear"), 1)
            eng.memset(zeros[:, :], 0.0).then_inc(S("cst"), 1)
            eng.memset(mhalf[:, :], -0.5).then_inc(S("cst"), 1)
            eng.memset(ident[:, :], 0.0).then_inc(S("cst"), 1)
            eng.memset(causal[:, :], 0.0).then_inc(S("cst"), 1)
            eng.memset(headm[:, :], 1.0).then_inc(S("cst"), 1)
            eng.memset(carry[:, :, :], 1.0).then_inc(S("cst"), 1)
            eng.memset(kt[:, :, :, :], 0.0).then_inc(S("cst"), 1)
            eng.memset(vv[:, :, :, :, :], 0.0).then_inc(S("cst"), 1)
            eng.memset(hnT[:, :, :], 0.0).then_inc(S("cst"), 1)
            eng.wait_ge(S("cst"), 9)
            done = 0

            def masked(tile, keep, fill, base, step, channel):
                nonlocal done
                if done:
                    eng.wait_ge(S("masks"), done)
                eng.affine_select(out=tile, in_=tile, compare_op=keep, fill=fill, base=base,
                                  pattern=[[step, tile.shape[1]]], channel_multiplier=channel).then_inc(S("masks"), 1)
                done += 1

            masked(ident[:, :], ALU.not_equal, 1.0, 0, -1, 1)
            masked(headm[:, :], ALU.is_ge, 0.0, 0, -HK, 1)
            masked(headm[:, :], ALU.is_ge, 0.0, HK - 1, HK, -1)
            for b in range(2):
                half = causal[64 * b:64 * b + 64, :]
                masked(half[:, 0:NPATCH], ALU.is_gt, 1.0, 0, -1, 1)
                masked(half, ALU.not_equal, 1.0, -NPATCH, 0, 1)
            eng.wait_ge(S("masks"), done)
            eng.memset(carry[:, :, 0:1], 0.0).then_inc(S("masks"), 1)
            eng.memset(carry[:, :, NPATCH:T], 0.0).then_inc(S("masks"), 1)
            eng.wait_ge(S("masks"), NMASK)

            def power(dst, src, n, name):
                eng.tensor_tensor(dst, src, mhalf[0:src.shape[0], 0:n], ALU.pow).then_inc(S(name), 1)

            def tick(t, u, has, first):
                if has(3):
                    eng.wait_ge(S("mse"), t - 3 + 1)
                    power(rso[:, :], mse[:, :], 2 * H, "rso")
                if has(0):
                    eng.wait_ge(S("ve0"), t + 1)
                    power(rs0[0:PROWS, :], ve[0:PROWS, 0:1], 1, "rs0")
                    eng.wait_ge(S("ve1"), t + 1)
                    power(rs1[0:ROWS, :], ve[0:ROWS, 1:2], 1, "rs1")
                if has(1):
                    i = t - 1
                    eng.wait_ge(S("qt"), i + 1)
                    if first >= 3:
                        eng.wait_ge(S("scores"), i - 1)
                    for b in range(2):
                        eng.tensor_tensor(qx[:, 1 - u, b, :, :], qt[:, b, :].unsqueeze(1).to_broadcast([KD, H, T]),
                                          headm[:, :].unsqueeze(2).to_broadcast([KD, H, T]),
                                          ALU.mult).then_inc(S("qx"), 1)

            ticks(eng, tick)

        @block.scalar
        def _(eng):
            rowv = lambda v: v.rearrange("(o n) -> o n", o=1)
            for dst, src in ((tokb, tok_b), (gam, tok_gamma), (bet, tok_beta)):
                eng.dma_start(dst[:, :], rowv(src).to_broadcast([128, D])).then_inc(S("ld"), 16)
            eng.dma_start(h_res[PROWS:ROWS, :, :],
                          cls_tok.rearrange("a b d -> a (b d)").unsqueeze(1).to_broadcast([2, PAIRS, D])).then_inc(S("ld"), 16)
            for dst, src in ((wq, Wq), (wk, Wk), (wv, Wv), (wg, Wg), (wo, Wo), (wgk1, Wgk1)):
                eng.dma_start(dst[:, :, :], src.rearrange("(k p) n -> p k n", p=DH)).then_inc(S("ld"), 16)
            eng.dma_start(wgk2[:, :], Wgk2).then_inc(S("ld"), 16)
            eng.dma_start(bgk[:, :], bgk2.rearrange("(p o) -> p o", o=1)).then_inc(S("ld"), 16)
            for h in range(KD // HV):
                eng.dma_start(onw[h * HV:(h + 1) * HV, :], o_norm_w.rearrange("(p o) -> p o", o=1)).then_inc(S("ld"), 16)

            def tick(t, u, has, first):
                if has(1):
                    i = t - 1
                    eng.wait_ge(S("T1"), i + 1)
                    if first >= 2:
                        eng.wait_ge(S("proj"), i)
                    src = ps_T[0:DH, 0:2 * ROWS].rearrange("p (k c) -> p k c", k=2)
                    dst = hnT[:, :, 0:ROWS].rearrange("p k (b t) -> p k b t", b=2)
                    eng.activation(dst[:, :, :, 0:NPATCH], src[:, :, 0:PROWS].rearrange("p k (b t) -> p k b t", b=2),
                                   ACT.Copy).then_inc(S("hnT"), 1)
                    eng.activation(dst[:, :, :, NPATCH], src[:, :, PROWS:ROWS], ACT.Copy).then_inc(S("hnT"), 1)
                if has(3):
                    i = t - 3
                    eng.wait_ge(S("pv"), i + 1)
                    if first >= 4:
                        eng.wait_ge(S("ms"), i)
                    eng.activation(sq[:, :], ps_o[0:T, 0:2 * D], ACT.Square).then_inc(S("sq"), 1)
                if has(1):
                    i = t - 1
                    gk = ps_qkg[0:KD, 2 * ROWS:3 * ROWS]
                    eng.wait_ge(S("gkps"), i + 1)
                    if first >= 2:
                        eng.wait_ge(S("mz"), i)
                    eng.activation(zz[:, :], gk, ACT.Identity, bias=bgk[:, 0:1]).then_inc(S("zz"), 1)
                    eng.wait_ge(S("zz"), i + 1)
                    eng.activation(az[:, :], zz[:, :], ACT.Abs).then_inc(S("az"), 1)
                    eng.wait_ge(S("az"), i + 1)
                    eng.activation(ez[:, :], az[:, :], ACT.Exp, scale=-1.0).then_inc(S("ez"), 1)
                    eng.wait_ge(S("ez"), i + 1)
                    if first >= 2:
                        eng.wait_ge(S("gl"), i)
                    eng.activation(lz[:, :], ez[:, :], ACT.Ln, bias=1.0).then_inc(S("lz"), 1)
                    eng.wait_ge(S("proj"), i + 1)
                    if first >= 2:
                        eng.wait_ge(S("eg1"), i)
                    eng.activation(eg[:, :], ps_vg[0:DH, D:D + 2 * ROWS], ACT.Exp, scale=-1.0).then_inc(S("eg"), 1)
                    if first >= 3:
                        eng.wait_ge(S("pv"), i - 1)
                    for b in range(2):
                        eng.activation(vv[64 * b:64 * b + 64, 1 - u, :, b, :],
                                       ps_vg[64 * b:64 * b + 64, 0:D].rearrange("p (h v) -> p h v", h=H),
                                       ACT.Copy).then_inc(S("vv"), 1)
                    eng.wait_ge(S("dc"), i + 1)
                    if first >= 2:
                        eng.wait_ge(S("qt"), i)
                        eng.wait_ge(S("kt"), i)
                    flat = dc[:, :, :].rearrange("p b t -> p (b t)")
                    eng.activation(ek[:, :], flat, ACT.Exp, scale=-1.0 / GATE_DIV).then_inc(S("ek"), 1)
                    eng.activation(eq[:, :], flat, ACT.Exp, scale=1.0 / GATE_DIV).then_inc(S("eq"), 1)

            ticks(eng, tick)

        @block.vector
        def _(eng):
            eng.wait_ge(S("w_in"), 480)
            for n in range(4):
                a = stage[0:2 * KC, 0] if n == 0 else weff[:, :, :]
                if n:
                    eng.wait_ge(S("wsum"), n)
                eng.tensor_tensor(weff[:, :, :], a, stage[0:2 * KC, n + 1], ALU.add).then_inc(S("wsum"), 1)
            eng.wait_ge(S("wsum"), 4)
            eng.wait_ge(S("ld"), 16 * 18)
            eng.wait_ge(S("masks"), NMASK)
            eng.tensor_scalar(wo[:, :, :], wo[:, :, :], onw[:, 0:1], None, ALU.mult).then_inc(S("weff_done"), 1)
            eng.wait_ge(S("w1T"), 1)
            eng.tensor_copy(wgk1T[:, :, :], ps_T[0:LR, 0:D].rearrange("p (k c) -> p k c", k=2)).then_inc(S("w1Tc"), 1)
            eng.wait_ge(S("wgkps"), 1)
            eng.tensor_copy(wgk[:, :, :], ps_T[0:DH, 0:2 * KD].rearrange("p (k c) -> p k c", k=2)).then_inc(S("wgk"), 1)

            def norm_stats(src, rows, l, i):
                eng.bn_stats(st6[0:rows, l, :], src).then_inc(S(f"st{l}"), 1)
                hold(eng, f"st{l}", i + 1, "dve")
                eng.bn_aggr(mv[0:rows, l, :], st6[0:rows, l, :]).then_inc(S(f"mv{l}"), 1)
                eng.wait_ge(S(f"mv{l}"), i + 1)
                eng.tensor_scalar(ve[0:rows, l:l + 1], mv[0:rows, l, 1:2], EPS, None, ALU.add).then_inc(S(f"ve{l}"), 1)

            def tick(t, u, has, first):
                if has(3):
                    i = t - 3
                    eng.wait_ge(S("sq"), i + 1)
                    eng.tensor_reduce(ms[:, :], sq[:, :].rearrange("p (g v) -> p g v", v=HV), AX.X,
                                      ALU.add).then_inc(S("ms"), 1)
                    eng.wait_ge(S("ms"), i + 1)
                    eng.tensor_scalar(mse[:, :], ms[:, :], 1.0 / HV, EPS, ALU.mult, ALU.add).then_inc(S("mse"), 1)
                if has(2):
                    i = t - 2
                    if first >= 4:
                        eng.wait_ge(S("pv"), i - 1)
                    eng.wait_ge(S("scores"), i + 1)
                    for n, bank in enumerate((ps_sa, ps_sb)):
                        eng.tensor_tensor(att[:, u, 6 * n:6 * n + 6, :],
                                          bank[:, 0:300].rearrange("p (h t) -> p h t", h=6),
                                          causal[:, :].unsqueeze(1).to_broadcast([128, 6, T]),
                                          ALU.mult).then_inc(S("att"), 1)
                if has(3):
                    i = t - 3
                    eng.wait_ge(S("rso"), i + 1)
                    if first >= 4:
                        eng.wait_ge(S("T2"), i)
                    eng.tensor_tensor(on[:, :, :].rearrange("p b (h v) -> p h b v", h=H),
                                      ps_o[0:T, 0:2 * D].rearrange("p (h b v) -> p h b v", h=H, b=2),
                                      rso[:, :].rearrange("p (h b) -> p h b", h=H).unsqueeze(3).to_broadcast([T, H, 2, HV]),
                                      ALU.mult).then_inc(S("on"), 1)
                if has(0):
                    i = t
                    eng.wait_ge(S("tok"), i + 1)
                    eng.tensor_tensor(s0[0:PROWS, :], ps_tok[0:PROWS, 0:D], tokb[0:PROWS, :], ALU.add).then_inc(S("s0"), 1)
                    hold(eng, "s0", i + 1, "dve")
                    norm_stats(s0[0:PROWS, :], PROWS, 0, i)
                if has(3):
                    i = t - 3
                    eng.wait_ge(S("T2"), i + 1)
                    if first >= 5:
                        eng.wait_ge(S("wo"), i - 1)
                    src = ps_T[0:DH, 256:256 + 2 * ROWS].rearrange("p (k b t) -> p k b t", k=2, b=2)
                    gv = gate[:, 1 - u, :, :].rearrange("p k (b t) -> p k b t", b=2)
                    dst = oT[:, 1 - u, :, :]
                    eng.tensor_tensor(dst[:, :, 0:PROWS].rearrange("p k (b t) -> p k b t", b=2), src[:, :, :, 0:NPATCH],
                                      gv[:, :, :, 0:NPATCH], ALU.mult).then_inc(S("oT"), 1)
                    eng.tensor_tensor(dst[:, :, PROWS:ROWS], src[:, :, :, NPATCH], gv[:, :, :, NPATCH],
                                      ALU.mult).then_inc(S("oT"), 1)
                if has(0):
                    i = t
                    eng.wait_ge(S("rs0"), i + 1)
                    eng.tensor_scalar(xn0[0:PROWS, :], s0[0:PROWS, :], mv[0:PROWS, 0, 0:1], rs0[0:PROWS, 0:1],
                                      ALU.subtract, ALU.mult).then_inc(S("xn0"), 1)
                    eng.wait_ge(S("xn0"), i + 1)
                    eng.tensor_tensor(xg[0:PROWS, :], xn0[0:PROWS, :], gam[0:PROWS, :], ALU.mult).then_inc(S("xg"), 1)
                    eng.wait_ge(S("xg"), i + 1)
                    eng.tensor_tensor(h_res[0:PROWS, i, :], xg[0:PROWS, :], bet[0:PROWS, :], ALU.add).then_inc(S("h0"), 1)
                    hold(eng, "h0", i + 1, "dve")
                    norm_stats(h_res[0:ROWS, i, :], ROWS, 1, i)
                if has(1):
                    i = t - 1
                    eng.wait_ge(S("zz"), i + 1)
                    eng.tensor_scalar(mz[:, :], zz[:, :], 0.0, None, ALU.min).then_inc(S("mz"), 1)
                    eng.wait_ge(S("mz"), i + 1)
                    eng.wait_ge(S("lz"), i + 1)
                    eng.tensor_tensor(gl[:, :, :].rearrange("p b t -> p (b t)"), mz[:, :], lz[:, :],
                                      ALU.subtract).then_inc(S("gl"), 1)
                    eng.wait_ge(S("gl"), i + 1)
                    eng.tensor_tensor(gl[:, :, 0:1], gl[:, :, 0:1], gl[:, :, NPATCH:T], ALU.add).then_inc(S("gl2"), 1)
                    eng.wait_ge(S("gl2"), i + 1)
                    eng.tensor_tensor_scan(gs[:, :, :].rearrange("p b t -> p (b t)"),
                                           carry[:, :, :].rearrange("p b t -> p (b t)"),
                                           gl[:, :, :].rearrange("p b t -> p (b t)"), 0.0, ALU.mult,
                                           ALU.add).then_inc(S("gs"), 1)
                    eng.wait_ge(S("gs"), i + 1)
                    eng.tensor_tensor(dd[:, :, :], gs[:, :, :], gs[:, :, T // 2 - 1:T // 2].to_broadcast([KD, 2, T]),
                                      ALU.subtract).then_inc(S("dd"), 1)
                    eng.wait_ge(S("dd"), i + 1)
                    if first >= 2:
                        eng.wait_ge(S("eq"), i)
                    eng.tensor_scalar(dc[:, :, :], dd[:, :, :], -CLAMP, CLAMP, ALU.max, ALU.min).then_inc(S("dc"), 1)
                    eng.wait_ge(S("eg"), i + 1)
                    eng.tensor_scalar(eg1[:, :], eg[:, :], 1.0, None, ALU.add).then_inc(S("eg1"), 1)
                if has(0):
                    i = t
                    eng.wait_ge(S("rs1"), i + 1)
                    if first >= 1:
                        eng.wait_ge(S("T1"), i)
                    eng.tensor_scalar(xn[:, :], h_res[0:ROWS, i, :], mv[0:ROWS, 1, 0:1], rs1[0:ROWS, 0:1],
                                      ALU.subtract, ALU.mult).then_inc(S("xn"), 1)
                if has(1):
                    i = t - 1
                    eng.wait_ge(S("eg1"), i + 1)
                    eng.reciprocal(sg[:, :], eg1[:, :]).then_inc(S("sg"), 1)
                    eng.wait_ge(S("ek"), i + 1)
                    if first >= 3:
                        eng.wait_ge(S("scores"), i - 1)
                    eng.tensor_tensor(kt[:, 1 - u, :, 0:T], ps_qkg[0:KD, ROWS:2 * ROWS].rearrange("p (b t) -> p b t", b=2),
                                      ek[:, :].rearrange("p (b t) -> p b t", b=2), ALU.mult).then_inc(S("kt"), 1)
                    eng.wait_ge(S("eq"), i + 1)
                    if first >= 2:
                        eng.wait_ge(S("qx"), 2 * i)
                    eng.scalar_tensor_tensor(out=qt[:, :, :], in0=ps_qkg[0:KD, 0:ROWS].rearrange("p (b t) -> p b t", b=2),
                                             scalar=float(HK) ** -0.5, in1=eq[:, :].rearrange("p (b t) -> p b t", b=2),
                                             op0=ALU.mult, op1=ALU.mult).then_inc(S("qt"), 1)
                    eng.wait_ge(S("sg"), i + 1)
                    eng.wait_ge(S("vv"), 2 * i + 2)
                    eng.tensor_tensor(gate[:, 1 - u, :, :], ps_vg[0:DH, D:D + 2 * ROWS].rearrange("p (k c) -> p k c", k=2),
                                      sg[:, :].rearrange("p (k c) -> p k c", k=2), ALU.mult).then_inc(S("gate"), 1)
                if has(3):
                    i = t - 3
                    eng.wait_ge(S("wo"), i + 1)
                    eng.tensor_tensor(h_res[0:ROWS, i, :], h_res[0:ROWS, i, :], ps_wo[0:ROWS, 0:D],
                                      ALU.add).then_inc(S("h1"), 1)

            ticks(eng, tick)

        @block.tensor
        def _(eng):
            eng.wait_ge(S("weff_done"), 1)
            for k in range(2):
                last = eng.transpose(ps_T[0:LR, k * DH:(k + 1) * DH], wgk1[:, k, :], ident[0:DH, 0:DH])
            last.then_inc(S("w1T"), 1)
            eng.wait_ge(S("w1Tc"), 1)
            for k in range(2):
                last = eng.matmul(ps_T[0:DH, k * KD:(k + 1) * KD], wgk1T[:, k, :], wgk2[:, :], start=True, stop=True)
            last.then_inc(S("wgkps"), 1)
            eng.wait_ge(S("wgk"), 1)
            eng.wait_ge(S("img_clear"), 2)

            def tick(t, u, has, first):
                if has(1):
                    i = t - 1
                    eng.wait_ge(S("xn"), i + 1)
                    if first >= 2:
                        eng.wait_ge(S("hnT"), 2 * i)
                    for k in range(2):
                        last = eng.transpose(ps_T[0:DH, k * ROWS:(k + 1) * ROWS], xn[:, k * DH:(k + 1) * DH],
                                             ident[0:ROWS, 0:ROWS])
                    last.then_inc(S("T1"), 1)
                if has(3):
                    i = t - 3
                    eng.wait_ge(S("att"), 2 * i + 2)
                    eng.wait_ge(S("vv"), 2 * i + 2)
                    if first >= 4:
                        eng.wait_ge(S("on"), i)
                    for h in range(H):
                        last = eng.matmul(ps_o[0:T, h * 2 * HV:(h + 1) * 2 * HV], att[:, 1 - u, h, :],
                                          vv[:, 1 - u, h, :, :], start=True, stop=True)
                    last.then_inc(S("pv"), 1)
                if has(2):
                    i = t - 2
                    eng.wait_ge(S("qx"), 2 * i + 2)
                    eng.wait_ge(S("kt"), i + 1)
                    if first >= 3:
                        eng.wait_ge(S("att"), 2 * i)
                    for b in range(2):
                        for n, bank in enumerate((ps_sa, ps_sb)):
                            last = eng.matmul(bank[64 * b:64 * b + 64, 0:300], kt[:, u, b, :],
                                              qx[:, u, b, 6 * n:6 * n + 6, :], start=True, stop=True)
                    last.then_inc(S("scores"), 1)
                if has(0):
                    i = t
                    eng.wait_ge(S("img"), 32 * i + 32)
                    if first >= 1:
                        eng.wait_ge(S("s0"), i)
                    for v in range(HALF):
                        lhs = img[:, u, :, :, :].rearrange("p b y w -> p (b y w)")[:, v:v + PATCH * (PROWS - 1) + 1:PATCH]
                        last = eng.matmul(ps_tok[0:PROWS, 0:D], lhs, weff[:, v, :], start=(v == 0), stop=(v == HALF - 1))
                    last.then_inc(S("tok"), 1)
                if has(1):
                    i = t - 1
                    eng.wait_ge(S("hnT"), 2 * i + 2)
                    if first >= 2:
                        eng.wait_ge(S("qt"), i)
                        eng.wait_ge(S("kt"), i)
                    for slot, w in ((2, wgk), (1, wk), (0, wq)):
                        for k in range(2):
                            last = eng.matmul(ps_qkg[0:KD, slot * ROWS:(slot + 1) * ROWS], w[:, k, :], hnT[:, k, 0:ROWS],
                                              start=(k == 0), stop=(k == 1))
                    last.then_inc(S("gkps"), 1)
                    if first >= 2:
                        eng.wait_ge(S("gate"), i)
                        eng.wait_ge(S("vv"), 2 * i)
                    for m in range(2):
                        for k in range(2):
                            eng.matmul(ps_vg[0:DH, D + m * ROWS:D + (m + 1) * ROWS], wg[:, k, m * DH:(m + 1) * DH],
                                       hnT[:, k, 0:ROWS], start=(k == 0), stop=(k == 1))
                    for k in range(2):
                        for b in range(2):
                            last = eng.matmul(ps_vg[64 * b:64 * b + 64, 0:D], hnT[:, k, T * b:T * b + 64],
                                              wv[:, k, :], start=(k == 0), stop=(k == 1))
                    last.then_inc(S("proj"), 1)
                if has(3):
                    i = t - 3
                    hold(eng, "on", i + 1, "pe")
                    if first >= 4:
                        hold(eng, "oT", 2 * i, "pe")
                    for b in range(2):
                        for k in range(2):
                            c = 256 + k * ROWS + b * T
                            last = eng.transpose(ps_T[0:DH, c:c + T], on[:, b, k * DH:(k + 1) * DH], ident[0:T, 0:T])
                    last.then_inc(S("T2"), 1)
                    eng.wait_ge(S("oT"), 2 * i + 2)
                    if first >= 4:
                        eng.wait_ge(S("h1"), i)
                    for k in range(2):
                        last = eng.matmul(ps_wo[0:ROWS, 0:D], oT[:, 1 - u, k, :], wo[:, k, :], start=(k == 0), stop=(k == 1))
                    last.then_inc(S("wo"), 1)

            ticks(eng, tick)


def part2(K, f_know, r_know, W_fk, b_fk, W_rk, b_rk, emb_fk, emb_rk):
    nc, S, hold, know, ident, mhalf, psum = (K[k] for k in ("nc", "S", "hold", "know", "ident", "mhalf", "psum"))
    h1_d, out_d = K["h1_d"], K["out_d"]
    sorted_in = (K["xs_d"], K["hs_d"])
    sorted_out = (K["hp_d"], K["op_d"])
    width_in, width_out = (D, R), (R, D)
    NT4 = NG * GQ
    HT = NT4 // 2
    IDX, EXPS, ZS, REC = 0, 8, 16, 18

    with ExitStack() as ctx:
        def sb(name, shape, dt=F32):
            return ctx.enter_context(nc.sbuf_tensor(name, shape, dt))

        h1c = sb("h1c", [128, NTILE, D]); hn2 = sb("hn2", [128, NTILE, D])
        rank = sb("rank", [128, NTILE, 2 * NN], U16)
        rec = sb("rec", [128, REC]); recs = sb("recs", [128, NTILE, REC])
        wcat = sb("wcat", [DH, 2, 2 * DS]); bcat = sb("bcat", [2 * DS, 1])
        emb = sb("emb", [128, 2, 2 * DS]); embT = sb("embT", [2 * DS, 2, NN])
        esq = sb("esq", [128, DS]); ess = sb("ess", [128, 2]); enr = sb("enr", [128, 2]); einv = sb("einv", [128, 2])
        phalf = sb("phalf", [128, 2])
        colI = sb("colI", [128, NN], I32); col = sb("col", [128, NN]); colb = sb("colb", [128, NN], BF16)
        rowI = sb("rowI", [128, 2], I32); row = sb("row", [128, 2])
        before = sb("before", [128, 128], BF16)
        upto = sb("upto", [128, 128], BF16)
        onesf = sb("onesf", [128, NN])
        st6 = sb("st6b", [128, 6]); mv = sb("mvb", [128, 2]); ve = sb("veb", [128, 1]); rs = sb("rsb", [128, 1])
        xn2 = sb("xn2", [128, D]); hT2 = sb("hT2", [DH, 2, 128]); qT = sb("qT", [2 * DS, 128])
        lg = sb("lg", [128, 2, NN]); m8 = sb("m8", [128, 2, 8]); i8 = sb("i8", [128, 2, 8], U32)
        negm = sb("negm", [128, 2]); junk = sb("junk", [128, NN])
        oh = sb("oh", [128, TOPK, 2, NN], BF16)
        se = sb("se", [128, NTILE, 2]); zs = sb("zs", [128, NTILE, 2]); rw = sb("rw", [128, NTILE, 2])
        wts = sb("wts", [128, NTILE, 2, TOPK])
        cI = sb("cI", [128, 2, NN], I32); cS = sb("cS", [128, 2, NN], I32); ntl = sb("ntl", [128, 2, NN])
        incl = sb("incl", [128, 2, NN]); off0 = sb("off0", [128, 2, NN]); off = sb("off", [128, 2, NN])
        eidc = sb("eidc", [128, 2, 2]); eid = sb("eid", [1, 2, NT4], I32)
        ro = sb("ro", [128, NN]); pj = sb("pj", [128, NN]); posf = sb("posf", [128, TOPK])
        posI = sb("posI", [128, 2, 2, TOPK], I32); pos_all = sb("pos_all", [128, NTILE, 2, TOPK], I32)
        gposI = sb("gposI", [128, 2, TOPK], I32)
        rows_out = sb("rows_out", [128, 2, D])
        pjs = sb("pjs", [128, TOPK, NN])
        block = ctx.enter_context(nc.Block())

        N, T0 = NTILE, 5

        def ticks(eng, body, depth, n=N, t0=T0):
            for t in range(t0):
                body(t, t % 2, lambda d, t=t: 0 <= t - d < n, t)
            with eng.Fori(0, (n - t0) // 2) as j:
                for u in range(2):
                    body(t0 + u + 2 * j, (t0 + u) % 2, lambda d: True, t0)
            for t in range(n, n + depth):
                body(t, t % 2, lambda d, t=t: 0 <= t - d < n, t)

        G0 = 4
        free = hn2[:, :, :].rearrange("p n d -> p (n d)")
        spare = lambda n: free[:, n * 2 * GQ * D:(n + 1) * 2 * GQ * D].rearrange("p (u q d) -> p u q d", u=2, d=D)
        xg, eo, got = spare(0), spare(1), spare(2)
        free1 = h1c[:, :, :].rearrange("p n d -> p (n d)")
        xT = free1[:, 0:2 * GQ * 256].rearrange("p (u c) -> p u c", u=2)
        at = 2 * GQ * 256
        acc = free1[:, at:at + TOPK * D].rearrange("p (j d) -> p j d", d=D)
        at += TOPK * D
        resid = free1[:, at:at + 2 * D].rearrange("p (u d) -> p u d", d=D)

        def xg_of(r, u):
            return xg[:, u, :, :].rearrange("p q d -> p (q d)")[:, 0:GQ * width_in[r]].rearrange(
                "p (q d) -> p q d", q=GQ)

        def eo_of(r, u):
            return eo[:, u, :, :].rearrange("p q d -> p (q d)")[:, 0:GQ * width_out[r]].rearrange(
                "p (q d) -> p q d", q=GQ)

        @block.sync
        def _(eng):
            eng.dma_start(h1c[:, :, :], h1_d.rearrange("(n p) d -> p n d", p=128)).then_inc(S("h1c"), 16)
            for half in range(2):
                eng.dma_start(know[0:DH, TAIL * 2 * R:].rearrange("p (n k r) -> p n k r", k=2, r=R)[:, :, half, :],
                              f_know[TAIL:NN, half * DH:(half + 1) * DH, :].rearrange("n p r -> p n r")
                              ).then_inc(S("know2"), 16)

            def group_rows(dram, g):
                return dram[bass.ds(g * (GQ * 128), GQ * 128), :].rearrange("(q p) d -> p q d", p=128)

            for r in range(2):
                for u in range(2):
                    eng.wait_ge(S(f"scat{r}{u}"), 64 * ((N + 1 - u) // 2))

                def tick(t, u, has, first, r=r):
                    if has(0):
                        if first >= 2:
                            hold(eng, f"xTp{r}", t - 1, "sp")
                        eng.dma_start(xg_of(r, u), group_rows(sorted_in[r], t)).then_inc(S(f"rows_in{r}{u}"), 16)
                    if has(2):
                        g = t - 2
                        hold(eng, f"eoA{r}", g + 1, "sp")
                        hold(eng, f"eoV{r}", g + 1, "sp")
                        eng.dma_start(group_rows(sorted_out[r], g), eo_of(r, u)).then_inc(S(f"rows_out{r}{u}"), 16)

                ticks(eng, tick, 2, NG, G0)
                if r == 0:
                    eng.wait_ge(S("prod0"), NG)
                    for c in range(4):
                        n0 = c * (NN // 4)
                        eng.dma_start(know[:, n0 * D:(n0 + NN // 4) * D].rearrange("p (n d) -> p n d", d=D),
                                      r_know[n0:n0 + NN // 4].rearrange("n r d -> r n d")).then_inc(S("rknow"), 16)

            def tick(t, u, has, first):
                if has(0):
                    if first >= 2:
                        hold(eng, "y", t - 1, "sp")
                    eng.dma_start(resid[:, u, :], h1_d[bass.ds(t * 128, 128), :]).then_inc(S(f"resid{u}"), 16)
                if has(1):
                    i = t - 1
                    hold(eng, "y", i + 1, "sp")
                    eng.dma_start(out_d[bass.ds(i * 128, 128), :], rows_out[:, 1 - u, :]).then_inc(S(f"out{1 - u}"), 16)

            ticks(eng, tick, 1)
            for u in range(2):
                eng.wait_ge(S(f"out{u}"), 16 * ((N + 1 - u) // 2))

        @block.gpsimd
        def _(eng):
            eng.memset(emb[:, :, :], 0.0).then_inc(S("emb0"), 1)
            eng.memset(phalf[:, :], 0.5).then_inc(S("cst2"), 1)
            eng.memset(onesf[:, :], 1.0).then_inc(S("cst2"), 1)
            eng.memset(before[:, :], 1.0).then_inc(S("cst2"), 1)
            eng.memset(upto[:, :], 1.0).then_inc(S("cst2"), 1)
            eng.iota(colI[:, :], pattern=[[1, NN]], base=0, channel_multiplier=0).then_inc(S("cst2"), 1)
            eng.iota(rowI[:, :], pattern=[[HT, 2]], base=0, channel_multiplier=1).then_inc(S("cst2"), 1)
            eng.wait_ge(S("cst2"), 6)
            eng.affine_select(out=before[:, :], in_=before[:, :], compare_op=ALU.is_gt, fill=0.0, base=0,
                              pattern=[[1, 128]], channel_multiplier=-1).then_inc(S("cst2"), 1)
            eng.wait_ge(S("cst2"), 7)
            eng.affine_select(out=upto[:, :], in_=upto[:, :], compare_op=ALU.is_ge, fill=0.0, base=0,
                              pattern=[[-1, 128]], channel_multiplier=1).then_inc(S("cst2"), 1)
            eng.wait_ge(S("cst2"), 8)
            eng.wait_ge(S("ess"), 2)
            eng.tensor_tensor(enr[:, :], ess[:, :], phalf[:, :], ALU.pow).then_inc(S("enr"), 1)

            def tick(t, u, has, first):
                if has(0):
                    eng.wait_ge(S("veb"), t + 1)
                    eng.tensor_tensor(rs[:, :], ve[:, :], mhalf[:, 0:1], ALU.pow).then_inc(S("rsb"), 1)

            ticks(eng, tick, 2)

            eng.wait_ge(S("ordered"), 1)

            def scatter(r, u, n_pos, n_rows, row_sem, dram, width):
                hold(eng, f"pos{r}", n_pos, "pool")
                hold(eng, row_sem, n_rows, "pool")
                for j in range(TOPK):
                    eng.indirect_dma_start(
                        out=dram, out_offset=bass.IndirectOffsetOnAxis(ap=posI[:, r, u, j:j + 1], axis=0),
                        in_=rows_out[:, u, 0:width], in_offset=None).then_inc(S(f"scat{r}{u}"), 16)

            def gather(u, dram, width, sem):
                for j in range(TOPK):
                    eng.indirect_dma_start(
                        out=got[:, u, j, 0:width], out_offset=None, in_=dram,
                        in_offset=bass.IndirectOffsetOnAxis(ap=gposI[:, u, j:j + 1], axis=0)).then_inc(S(f"{sem}{u}"), 16)

            def tick(t, u, has, first):
                if has(0):
                    scatter(0, u, t + 1, t + 1, "staged", sorted_in[0], D)

            ticks(eng, tick, 0)

            for u in range(2):
                eng.wait_ge(S(f"rows_out0{u}"), 16 * (NG // 2))

            def tick(t, u, has, first):
                if has(0):
                    hold(eng, "gpos", t + 1, "pool")
                    if first >= 2:
                        hold(eng, "mix", 4 * (t - 1), "pool")
                    gather(u, sorted_out[0], R, "gath")
                if has(1):
                    scatter(1, 1 - u, t, 4 * t, "mix", sorted_in[1], R)

            ticks(eng, tick, 1)
            for u in range(2):
                eng.wait_ge(S(f"rows_out1{u}"), 16 * (NG // 2))

            def tick(t, u, has, first):
                if has(0):
                    hold(eng, "gpos", N + t + 1, "pool")
                    if first >= 2:
                        hold(eng, "y", t - 1, "pool")
                    gather(u, sorted_out[1], D, "gathy")

            ticks(eng, tick, 0)

        @block.scalar
        def _(eng):
            eng.wait_ge(S("emb0"), 1)
            for r, (W, bias, e) in enumerate(((W_fk, b_fk, emb_fk), (W_rk, b_rk, emb_rk))):
                cols = slice(r * DS, (r + 1) * DS)
                eng.dma_start(wcat[:, :, cols], W.rearrange("(k p) n -> p k n", p=DH)).then_inc(S("ld2"), 16)
                eng.dma_start(bcat[cols, :], bias.rearrange("(p o) -> p o", o=1)).then_inc(S("ld2"), 16)
                eng.dma_start(emb[:, r, cols], e).then_inc(S("ld2"), 16)
            eng.wait_ge(S("ld2"), 96)
            for r in range(2):
                if r:
                    eng.wait_ge(S("ess"), 1)
                eng.activation(esq[:, :], emb[:, r, r * DS:(r + 1) * DS], ACT.Square,
                               accum_out=ess[:, r:r + 1]).then_inc(S("ess"), 1)
            eng.wait_ge(S("embTp"), 1)
            eng.activation(embT[:, :, :], psum[4][:, 0:2 * NN].rearrange("p (r n) -> p r n", r=2),
                           ACT.Copy).then_inc(S("embT"), 1)

            def tick(t, u, has, first):
                if has(2):
                    i = t - 2
                    eng.wait_ge(S("rankp"), i + 1)
                    eng.activation(rank[:, i, :], psum[0][:, 0:2 * NN], ACT.Copy).then_inc(S("rank"), 1)
                if has(1):
                    i = t - 1
                    eng.wait_ge(S("lgp"), i + 1)
                    if first >= 2:
                        eng.wait_ge(S("idx"), 2 * i)
                    eng.activation(lg[:, :, :], psum[1][:, 0:2 * NN].rearrange("p (r n) -> p r n", r=2),
                                   ACT.Copy).then_inc(S("lg"), 1)
                if has(0):
                    eng.wait_ge(S("T3"), t + 1)
                    if first >= 1:
                        eng.wait_ge(S("qp"), t)
                    eng.activation(hT2[:, :, :], psum[2][0:DH, 0:256].rearrange("p (k c) -> p k c", k=2),
                                   ACT.Copy).then_inc(S("hT2"), 1)
                    eng.activation(hn2[:, t, :], xn2[:, :], ACT.Copy).then_inc(S("hn2"), 1)
                if has(1):
                    i = t - 1
                    eng.wait_ge(S("negm"), i + 1)
                    if first >= 2:
                        eng.wait_ge(S("recs"), i)
                    for r in range(2):
                        if r or first >= 2:
                            eng.wait_ge(S("esum"), 2 * i + r)
                        eng.activation(junk[:, :], lg[:, r, :], ACT.Exp, bias=negm[:, r:r + 1],
                                       accum_out=rec[:, ZS + r:ZS + r + 1]).then_inc(S("esum"), 1)
                    for r in range(2):
                        eng.activation(rec[:, EXPS + 4 * r:EXPS + 4 * r + 4], m8[:, r, 0:TOPK], ACT.Exp,
                                       bias=negm[:, r:r + 1]).then_inc(S("e4"), 1)
                if has(0):
                    eng.wait_ge(S("qp"), t + 1)
                    if first >= 1:
                        eng.wait_ge(S("lgp"), t)
                    eng.activation(qT[:, :], psum[3][:, 0:128], ACT.Identity, bias=bcat[:, 0:1]).then_inc(S("qT"), 1)

            ticks(eng, tick, 2)

            def tick(t, u, has, first):
                if has(0):
                    if first >= 2:
                        eng.wait_ge(S(f"scat0{u}"), 64 * (t // 2) if isinstance(t, int) else (t - u) * 32)
                    eng.activation(rows_out[:, u, :], hn2[:, t, :], ACT.Copy).then_inc(S("staged"), 1)

            ticks(eng, tick, 0)

            for r in range(2):
                def tick(t, u, has, first, r=r):
                    if has(0):
                        eng.wait_ge(S(f"xTp{r}"), t + 1)
                        if first >= 2:
                            eng.wait_ge(S(f"prod{r}"), t - 1)
                        eng.activation(xT[0:DH if r == 0 else 128, u, 0:512 if r == 0 else 256],
                                       psum[0][0:DH if r == 0 else 128, 0:512 if r == 0 else 256],
                                       ACT.Copy).then_inc(S(f"xTA{r}"), 1)
                    if has(1):
                        g = t - 1
                        eng.wait_ge(S(f"prod{r}"), g + 1)
                        if first >= 3:
                            eng.wait_ge(S(f"rows_out{r}{1 - u}"), (g // 2) * 16 if isinstance(g, int) else (g - 1 + u) * 8)
                        eng.activation(eo_of(r, 1 - u)[:, 0:2, :],
                                       psum[2 + 2 * (1 - u)][:, 0:2 * width_out[r]].rearrange("p (q d) -> p q d", q=2),
                                       ACT.Copy).then_inc(S(f"eoA{r}"), 1)

                ticks(eng, tick, 1, NG, G0)

        @block.vector
        def _(eng):
            eng.wait_ge(S("cst2"), 8)
            eng.tensor_copy(col[:, :], colI[:, :]).then_inc(S("cst3"), 1)
            eng.tensor_copy(colb[:, :], colI[:, :]).then_inc(S("cst3"), 1)
            eng.tensor_copy(row[:, :], rowI[:, :]).then_inc(S("cst3"), 1)
            eng.wait_ge(S("enr"), 1)
            eng.tensor_scalar(einv[:, :], enr[:, :], 1e-8, None, ALU.add).then_inc(S("einv"), 1)
            eng.wait_ge(S("einv"), 1)
            eng.reciprocal(enr[:, :], einv[:, :]).then_inc(S("einv"), 1)
            eng.wait_ge(S("einv"), 2)
            for r in range(2):
                eng.tensor_scalar(emb[:, r, :], emb[:, r, :], enr[:, r:r + 1], None, ALU.mult).then_inc(S("embn"), 1)
            eng.wait_ge(S("cst3"), 3)
            eng.wait_ge(S("h1c"), 16)

            def tick(t, u, has, first):
                if has(0):
                    eng.bn_stats(st6[:, :], h1c[:, t, :]).then_inc(S("stb"), 1)
                    hold(eng, "stb", t + 1, "dve")
                    eng.bn_aggr(mv[:, :], st6[:, :]).then_inc(S("mvb"), 1)
                    eng.wait_ge(S("mvb"), t + 1)
                    eng.tensor_scalar(ve[:, :], mv[:, 1:2], EPS, None, ALU.add).then_inc(S("veb"), 1)
                if has(1):
                    i = t - 1
                    hold(eng, "lg", i + 1, "dve")
                    if first >= 2:
                        hold(eng, "e4", 2 * i, "dve")
                    for r in range(2):
                        eng.max(m8[:, r, :], lg[:, r, :]).then_inc(S("m8"), 1)
                    eng.wait_ge(S("m8"), 2 * i + 2)
                    eng.tensor_scalar(negm[:, :], m8[:, :, 0], -1.0, None, ALU.mult).then_inc(S("negm"), 1)
                    for r in range(2):
                        eng.max_index(i8[:, r, :], m8[:, r, :], lg[:, r, :]).then_inc(S("idx"), 1)
                    eng.wait_ge(S("idx"), 2 * i + 2)
                    if first >= 2:
                        eng.wait_ge(S("recs"), i)
                    eng.tensor_copy(rec[:, IDX:IDX + 8].rearrange("p (r j) -> p r j", r=2),
                                    i8[:, :, 0:TOPK]).then_inc(S("recx"), 1)
                if has(0):
                    eng.wait_ge(S("rsb"), t + 1)
                    if first >= 1:
                        eng.wait_ge(S("hn2"), t)
                        eng.wait_ge(S("T3"), t)
                    eng.tensor_scalar(xn2[:, :], h1c[:, t, :], mv[:, 0:1], rs[:, 0:1], ALU.subtract,
                                      ALU.mult).then_inc(S("xn2"), 1)
                if has(1):
                    i = t - 1
                    eng.wait_ge(S("recx"), i + 1)
                    if first >= 2:
                        eng.wait_ge(S("ranku"), i)
                    for r in range(2):
                        for j in range(TOPK):
                            eng.tensor_scalar(oh[:, j, r, :], colb[:, :], rec[:, IDX + 4 * r + j:IDX + 4 * r + j + 1],
                                              None, ALU.is_equal).then_inc(S("oh"), 1)
                    eng.wait_ge(S("e4"), 2 * i + 2)
                    eng.tensor_copy(recs[:, i, :], rec[:, :]).then_inc(S("recs"), 1)

            ticks(eng, tick, 2)

            eng.wait_ge(S("recs"), N)
            e_all = recs[:, :, EXPS:EXPS + 8].rearrange("p n (r j) -> p n r j", r=2)
            eng.tensor_reduce(se[:, :, :], e_all, AX.X, ALU.add).then_inc(S("w"), 1)
            eng.wait_ge(S("w"), 1)
            eng.scalar_tensor_tensor(out=zs[:, :, :], in0=recs[:, :, ZS:REC], scalar=1e-8, in1=se[:, :, :],
                                     op0=ALU.mult, op1=ALU.add).then_inc(S("w"), 1)
            eng.wait_ge(S("w"), 2)
            eng.reciprocal(rw[:, :, :], zs[:, :, :]).then_inc(S("w"), 1)
            eng.wait_ge(S("w"), 3)
            for r in range(2):
                eng.tensor_tensor(wts[:, :, r, :], e_all[:, :, r, :],
                                  rw[:, :, r:r + 1].to_broadcast([128, N, TOPK]), ALU.mult).then_inc(S("w"), 1)
            eng.wait_ge(S("ranku"), N)
            eng.wait_ge(S("rank"), N)
            eng.tensor_scalar(cI[:, :, :], psum[0][:, 0:2 * NN].rearrange("p (r n) -> p r n", r=2), 127.0, None,
                              ALU.add).then_inc(S("ord"), 1)
            eng.wait_ge(S("ord"), 1)
            eng.tensor_scalar(cS[:, :, :], cI[:, :, :], 7, None, ALU.logical_shift_right).then_inc(S("ord"), 1)
            eng.wait_ge(S("ord"), 2)
            eng.tensor_copy(ntl[:, :, :], cS[:, :, :]).then_inc(S("ord"), 1)
            eng.wait_ge(S("ord"), 3)
            for r in range(2):
                eng.tensor_tensor_scan(incl[:, r, :], onesf[:, :], ntl[:, r, :], 0.0, ALU.mult,
                                       ALU.add).then_inc(S("ord"), 1)
            eng.wait_ge(S("ord"), 5)
            eng.tensor_tensor(off0[:, :, :], incl[:, :, :], ntl[:, :, :], ALU.subtract).then_inc(S("ord"), 1)
            eng.wait_ge(S("ord"), 6)
            eng.tensor_scalar(off[:, :, :], off0[:, :, :], 128.0, None, ALU.mult).then_inc(S("ord"), 1)
            n = 7
            for r in range(2):
                for hh in range(2):
                    eng.wait_ge(S("ord"), n)
                    eng.scalar_tensor_tensor(out=pj[0:HT, :], in0=incl[0:HT, r, :], scalar=row[0:HT, hh:hh + 1],
                                             in1=onesf[0:HT, :], op0=ALU.is_le, op1=ALU.mult,
                                             accum_out=eidc[0:HT, r, hh:hh + 1]).then_inc(S("ord"), 1)
                    n += 1
            eng.wait_ge(S("ord"), n)
            eng.wait_ge(S("eidp"), 1)
            eng.tensor_scalar(eid[:, :, :], psum[1][0:1, 0:2 * NT4].rearrange("p (r n) -> p r n", r=2),
                              float(NN - 1), None, ALU.min).then_inc(S("ordered"), 1)
            eng.wait_ge(S("w"), 5)

            def positions(r, i, u, i_done):
                eng.wait_ge(S("ro"), N * r + i_done) if i_done is not None or r else None
                eng.tensor_tensor(ro[:, :], rank[:, i, r * NN:(r + 1) * NN], off[:, r, :], ALU.add).then_inc(S("ro"), 1)
                eng.wait_ge(S("ro"), N * r + i + 1)
                for j in range(TOPK):
                    eng.scalar_tensor_tensor(out=pjs[:, j, :], in0=col[:, :],
                                             scalar=recs[:, i, IDX + 4 * r + j:IDX + 4 * r + j + 1], in1=ro[:, :],
                                             op0=ALU.is_equal, op1=ALU.mult,
                                             accum_out=posf[:, j:j + 1]).then_inc(S("pj"), 1)
                eng.wait_ge(S("pj"), 4 * (N * r + i + 1))
                eng.tensor_copy(posI[:, r, u, :], posf[:, :]).then_inc(S(f"pos{r}"), 1)
                eng.tensor_copy(pos_all[:, i, r, :], posf[:, :]).then_inc(S("pall"), 1)

            def tick(t, u, has, first):
                if has(0):
                    if first >= 2:
                        eng.wait_ge(S(f"scat0{u}"), 64 * (t // 2) if isinstance(t, int) else (t - u) * 32)
                    positions(0, t, u, t if first >= 1 else None)

            ticks(eng, tick, 0)

            def expert(r):
                def tick(t, u, has, first):
                    if has(0):
                        eng.wait_ge(S(f"xTp{r}"), t + 1)
                        if first >= 2:
                            eng.wait_ge(S(f"prod{r}"), t - 1)
                        if r == 0:
                            eng.tensor_copy(xT[0:DH, u, 512:1024], psum[1][0:DH, :]).then_inc(S("xTV0"), 1)
                        else:
                            eng.tensor_copy(xT[:, u, 256:512], psum[1][:, 0:256]).then_inc(S("xTV1"), 1)
                    if has(1):
                        g = t - 1
                        eng.wait_ge(S(f"prod{r}"), g + 1)
                        if first >= 3:
                            eng.wait_ge(S(f"rows_out{r}{1 - u}"), (g // 2) * 16 if isinstance(g, int) else (g - 1 + u) * 8)
                        eng.tensor_copy(eo_of(r, 1 - u)[:, 2:4, :],
                                        psum[3 + 2 * (1 - u)][:, 0:2 * width_out[r]].rearrange("p (q d) -> p q d", q=2)
                                        ).then_inc(S(f"eoV{r}"), 1)

                ticks(eng, tick, 1, NG, G0)

            expert(0)
            for u in range(2):
                eng.wait_ge(S(f"scat0{u}"), 64 * ((N + 1 - u) // 2))
            eng.wait_ge(S("pall"), N)

            def tick(t, u, has, first):
                if has(0):
                    if first >= 2:
                        eng.wait_ge(S(f"gath{u}"), 64 * (t // 2) if isinstance(t, int) else (t - u) * 32)
                    eng.tensor_copy(gposI[:, u, :], pos_all[:, t, 0, :]).then_inc(S("gpos"), 1)
                    if first >= 2:
                        eng.wait_ge(S(f"scat1{u}"), 64 * (t // 2) if isinstance(t, int) else (t - u) * 32)
                    positions(1, t, u, t)
                if has(1):
                    i, v = t - 1, 1 - u
                    eng.wait_ge(S(f"gath{v}"), 64 * (i // 2) + 64 if isinstance(i, int) else (i - v) * 32 + 64)
                    for j in range(TOPK):
                        w = wts[:, i, 0, j:j + 1]
                        if j == 0:
                            eng.tensor_scalar(acc[:, 0, 0:R], got[:, v, 0, 0:R], w, None, ALU.mult).then_inc(S("mix"), 1)
                        else:
                            eng.wait_ge(S("mix"), 4 * i + j)
                            dst = rows_out[:, v, 0:R] if j == TOPK - 1 else acc[:, j, 0:R]
                            eng.scalar_tensor_tensor(out=dst, in0=got[:, v, j, 0:R], scalar=w, in1=acc[:, j - 1, 0:R],
                                                     op0=ALU.mult, op1=ALU.add).then_inc(S("mix"), 1)

            ticks(eng, tick, 1)
            expert(1)
            for u in range(2):
                eng.wait_ge(S(f"scat1{u}"), 64 * ((N + 1 - u) // 2))
            eng.wait_ge(S("pall"), 2 * N)

            def tick(t, u, has, first):
                if has(0):
                    if first >= 2:
                        eng.wait_ge(S(f"gathy{u}"), 64 * (t // 2) if isinstance(t, int) else (t - u) * 32)
                    eng.tensor_copy(gposI[:, u, :], pos_all[:, t, 1, :]).then_inc(S("gpos"), 1)
                if has(1):
                    i, v = t - 1, 1 - u
                    eng.wait_ge(S(f"gathy{v}"), 64 * (i // 2) + 64 if isinstance(i, int) else (i - v) * 32 + 64)
                    if first >= 3:
                        eng.wait_ge(S(f"out{v}"), 16 * (i // 2) if isinstance(i, int) else (i - v) * 8)
                    eng.wait_ge(S(f"resid{v}"), 16 * (i // 2) + 16 if isinstance(i, int) else (i - v) * 8 + 16)
                    for j in range(TOPK):
                        if j or first >= 2:
                            eng.wait_ge(S("ymix"), 4 * i + j)
                        dst = rows_out[:, v, :] if j == TOPK - 1 else acc[:, j, :]
                        src = resid[:, v, :] if j == 0 else acc[:, j - 1, :]
                        ins = eng.scalar_tensor_tensor(out=dst, in0=got[:, v, j, :], scalar=wts[:, i, 1, j:j + 1],
                                                       in1=src, op0=ALU.mult, op1=ALU.add)
                        ins.then_inc(S("ymix"), 1)
                    eng.wait_ge(S("ymix"), 4 * i + 4)
                    eng.sem_inc(S("y"), 1)

            ticks(eng, tick, 1)

        @block.tensor
        def _(eng):
            eng.wait_ge(S("embn"), 2)
            for r in range(2):
                last = eng.transpose(psum[4][:, r * NN:(r + 1) * NN], emb[:, r, :], ident[:, :])
            last.then_inc(S("embTp"), 1)
            eng.wait_ge(S("embT"), 1)
            eng.wait_ge(S("ld2"), 96)

            def tick(t, u, has, first):
                if has(2):
                    i = t - 2
                    eng.wait_ge(S("oh"), 8 * i + 8)
                    for j in range(TOPK):
                        last = eng.matmul(psum[0][:, 0:2 * NN], before[:, :], oh[:, j, :, :],
                                          start=(first == 2 and j == 0), stop=False, skip_group_check=True)
                    last.then_inc(S("rankp"), 1)
                    eng.wait_ge(S("rank"), i + 1)
                    for j in range(TOPK):
                        last = eng.matmul(psum[0][:, 0:2 * NN], upto[:, :], oh[:, j, :, :],
                                          start=False, stop=False, skip_group_check=True)
                    last.then_inc(S("ranku"), 1)
                if has(1):
                    i = t - 1
                    eng.wait_ge(S("qT"), i + 1)
                    if first >= 2:
                        eng.wait_ge(S("lg"), i)
                    eng.matmul(psum[1][:, 0:2 * NN], qT[:, :], embT[:, :, :], start=True, stop=True).then_inc(S("lgp"), 1)
                if has(0):
                    hold(eng, "xn2", t + 1, "pe")
                    if first >= 1:
                        hold(eng, "hT2", t, "pe")
                    for k in range(2):
                        last = eng.transpose(psum[2][0:DH, k * 128:(k + 1) * 128], xn2[:, k * DH:(k + 1) * DH], ident[:, :])
                    last.then_inc(S("T3"), 1)
                    eng.wait_ge(S("hT2"), t + 1)
                    if first >= 1:
                        eng.wait_ge(S("qT"), t)
                    for k in range(2):
                        last = eng.matmul(psum[3][:, 0:128], wcat[:, k, :], hT2[:, k, :], start=(k == 0), stop=(k == 1))
                    last.then_inc(S("qp"), 1)

            ticks(eng, tick, 2)
            eng.wait_ge(S("ord"), 11)
            for r in range(2):
                for hh in range(2):
                    at = r * NT4 + hh * HT
                    last = eng.matmul(psum[1][0:1, at:at + HT], eidc[0:HT, r, hh:hh + 1], ident[0:HT, 0:HT],
                                      start=True, stop=True)
            last.then_inc(S("eidp"), 1)
            eng.wait_ge(S("ordered"), 1)

            for r in range(2):
                if r == 0:
                    eng.wait_ge(S("know2"), 32)
                else:
                    eng.wait_ge(S("rknow"), 64)
                kd = DH if r == 0 else 128
                nk = 2 if r == 0 else 1
                wo = width_out[r]
                regs = [eng.alloc_register(f"neuron{r}{q}") for q in range(GQ)]

                def tick(t, u, has, first, r=r, kd=kd, nk=nk, wo=wo, regs=regs):
                    if has(0):
                        hold(eng, f"rows_in{r}{u}", 16 * (t // 2) + 16 if isinstance(t, int) else (t - u) * 8 + 16, "pe")
                        if first >= 1:
                            hold(eng, f"xTA{r}", t, "pe")
                            hold(eng, f"xTV{r}", t, "pe")
                        for q in range(GQ):
                            for k in range(nk):
                                at = (q % 2) * nk * 128 + k * 128
                                last = eng.transpose(psum[q // 2][0:kd, at:at + 128],
                                                     xg_of(r, u)[:, q, k * kd:(k + 1) * kd], ident[:, :])
                        last.then_inc(S(f"xTp{r}"), 1)
                    if has(1):
                        g, v = t - 1, 1 - u
                        eng.load(regs, eid[0:1, r, bass.ds(g * GQ, GQ)])
                        vals = [eng.snap(x, min_val=0, max_val=NN - 1) for x in regs]
                        for who in "AV":
                            eng.wait_ge(S(f"xT{who}{r}"), g + 1)
                            if first >= 3:
                                eng.wait_ge(S(f"eo{who}{r}"), g - 1)
                        for q in range(GQ):
                            for k in range(nk):
                                at = (q * nk + k) * 128
                                last = eng.matmul(psum[2 + 2 * v + q // 2][:, (q % 2) * wo:(q % 2 + 1) * wo],
                                                  xT[0:kd, v, at:at + 128],
                                                  know[0:kd, bass.ds(vals[q] * (nk * wo) + k * wo, wo)],
                                                  start=(k == 0), stop=(k == nk - 1))
                        last.then_inc(S(f"prod{r}"), 1)

                ticks(eng, tick, 1, NG, G0)


_INS = ["x", "cls_tok", "L0_tok_W", "L0_tok_b", "L0_tok_gamma", "L0_tok_beta", "L0_attn_Wq", "L0_attn_Wk",
        "L0_attn_Wv", "L0_attn_Wgk1", "L0_attn_Wgk2", "L0_attn_bgk2", "L0_attn_Wg", "L0_attn_o_norm_w",
        "L0_attn_Wo", "L0_ffn_f_know", "L0_ffn_r_know", "L0_ffn_W_fk", "L0_ffn_b_fk", "L0_ffn_W_rk",
        "L0_ffn_b_rk", "L0_ffn_emb_fk", "L0_ffn_emb_rk"]
_OUTS = [((B, T, D), "float32")]


def kernel(**inputs):
    import numpy as _np
    import concourse.bacc as _bacc
    from concourse import mybir as _mybir
    from concourse.bass_utils import run_bass_kernel_spmd as _run

    nc = _bacc.Bacc("TRN2", target_bir_lowering=False, num_devices=1)
    arrays, args = {}, []
    for name in _INS:
        a = _np.ascontiguousarray(inputs[name])
        arrays[f"in_{name}_dram"] = a
        args.append(nc.dram_tensor(f"in_{name}_dram", a.shape, _mybir.dt.from_np(a.dtype), kind="ExternalInput").ap())
    for i, (shape, dtype) in enumerate(_OUTS):
        dt = _mybir.dt.from_np(_np.dtype(dtype))
        args.append(nc.dram_tensor(f"out_{i}_dram", shape, dt, kind="ExternalOutput").ap())
    vit_kernel(nc, *args)
    r = _run(nc, [arrays], core_ids=[0])
    got = tuple(r.results[0][f"out_{i}_dram"] for i in range(len(_OUTS)))
    return got[0]
```

```python
from contextlib import ExitStack

import numpy as np
import concourse.bass as bass
from concourse import mybir
from concourse.alu_op_type import AluOpType as ALU

ACT = mybir.ActivationFunctionType
F32, BF16 = mybir.dt.float32, mybir.dt.bfloat16
I32, U32, U16 = mybir.dt.int32, mybir.dt.uint32, mybir.dt.uint16
AX = mybir.AxisListType
EXP_LN_SET = 6

B, C, HW, PATCH = 64, 3, 112, 16
GRID = HW // PATCH
NPATCH = GRID * GRID
T = NPATCH + 1
D, KD, H = 192, 96, 12
HK, HV = KD // H, D // H
LR = 16
DH = D // 2
PAIRS = B // 2
ROWS = 2 * T
PROWS = 2 * NPATCH
WIN = PATCH + 2
HALF = WIN // 2
KC = C * WIN
KHI = 64
XW = HW + 2
EPS = 1e-5
GATE_DIV = 16.0
CLAMP = 43.0 * GATE_DIV

NTOK = B * T
NTILE = NTOK // 128
NN, R, DS, TOPK = 128, 128, 64, 4
GQ = 4
MAXT = (NTOK * TOPK + NN * 127) // 128
NG = -(-MAXT // GQ)
NG += NG % 2
SLOTS = NG * GQ * 128
SH = ((1, 1), (2, 2), (2, 0), (0, 2), (0, 0))


def vit_kernel(nc, x, cls_tok, tok_W, tok_b, tok_gamma, tok_beta, Wq, Wk, Wv, Wgk1, Wgk2, bgk2, Wg,
               o_norm_w, Wo, f_know, r_know, W_fk, b_fk, W_rk, b_rk, emb_fk, emb_rk, out):
    h1_d = nc.dram_tensor("h1_d", [NTOK, D], F32, kind="Internal").ap()
    xs_d = nc.dram_tensor("xs_d", [SLOTS, D], F32, kind="Internal").ap()
    hp_d = nc.dram_tensor("hp_d", [SLOTS, R], F32, kind="Internal").ap()
    hs_d = nc.dram_tensor("hs_d", [SLOTS, R], F32, kind="Internal").ap()
    op_d = nc.dram_tensor("op_d", [SLOTS, D], F32, kind="Internal").ap()
    out_d = out.rearrange("b t d -> (b t) d")

    with ExitStack() as top:
        def sbt(name, shape, dt=F32):
            return top.enter_context(nc.sbuf_tensor(name, shape, dt))

        know = sbt("know", [128, NN * 2 * R])
        ident = sbt("ident", [128, 128])
        mhalf = sbt("mhalf", [128, 1])
        zeros = sbt("zeros", [128, ZW])
        psum = [top.enter_context(nc.psum_tensor(f"bank{i}", [128, 512], F32)) for i in range(8)]
        sems = {}

        def S(name):
            if name not in sems:
                sems[name] = top.enter_context(nc.semaphore(name))
            return sems[name]

        def hold(eng, name, value, who):
            eng.wait_ge(S(name), value)
            eng.sem_inc(S(f"passed_{who}"), 1)

        K = dict(nc=nc, S=S, hold=hold, zeros=zeros, know=know, ident=ident, mhalf=mhalf, psum=psum, h1_d=h1_d, xs_d=xs_d,
                 hp_d=hp_d, hs_d=hs_d, op_d=op_d, out_d=out_d)
        part1(K, x, cls_tok, tok_W, tok_b, tok_gamma, tok_beta, Wq, Wk, Wv, Wgk1, Wgk2, bgk2, Wg, o_norm_w, Wo,
              f_know)
        part2(K, f_know, r_know, W_fk, b_fk, W_rk, b_rk, emb_fk, emb_rk)


NCHUNK = (PAIRS - 2) // 2
ZW = 256
KCH = 5
NMASK = 9
TAIL = NCHUNK * KCH


def clear(eng, S, zeros, dst, at, n):
    flat = dst.rearrange("(p r) d -> p (r d)", p=128)
    eng.dma_start(flat[:, bass.ds(at * ZW, n * ZW)].rearrange("p (n m) -> p n m", n=n),
                  zeros[:, :].unsqueeze(1).to_broadcast([128, n, ZW])).then_inc(S("zeroed"), 16)


def part1(K, x, cls_tok, tok_W, tok_b, tok_gamma, tok_beta, Wq, Wk, Wv, Wgk1, Wgk2, bgk2, Wg, o_norm_w, Wo,
          f_know):
    nc, know, ident, mhalf, psum, zeros = (K[k] for k in ("nc", "know", "ident", "mhalf", "psum", "zeros"))
    h1_d, xs_d = K["h1_d"], K["xs_d"]
    with ExitStack() as ctx:
        def sb(name, shape, dt=F32):
            return ctx.enter_context(nc.sbuf_tensor(name, shape, dt))

        S, hold = K["S"], K["hold"]
        tail0 = TAIL * 2 * R
        h_res = know[:, tail0:tail0 + PAIRS * D].rearrange("p (i d) -> p i d", d=D)
        gate = know[0:DH, tail0 + PAIRS * D:tail0 + PAIRS * (D + 2 * ROWS)].rearrange("p (i k c) -> p i k c", k=2, c=ROWS)
        stage = know[:, 0:5 * HALF * D].rearrange("p (s v e) -> p s v e", s=5, v=HALF)
        weff = sb("weff", [KHI + KC, HALF, D])
        raw = sb("raw", [KC, 2, 2, GRID, XW])
        img = sb("img", [KHI + KC, 2, 2, GRID, HW])
        wq = sb("wq", [DH, 2, KD]); wk = sb("wk", [DH, 2, KD])
        wgk = sb("wgk", [DH, 2, KD]); wgk1T = sb("wgk1T", [LR, 2, DH])
        wgk1 = sb("wgk1", [DH, 2, LR]); wgk2 = sb("wgk2", [LR, KD])
        wv = sb("wv", [DH, 2, D]); wg = sb("wg", [DH, 2, D]); wo = sb("wo", [DH, 2, D])
        onw = sb("onw", [DH, 1]); bgk = sb("bgk", [KD, 1])
        tokb = sb("tokb", [128, D]); gam = sb("gam", [128, D]); bet = sb("bet", [128, D])
        causal = sb("causal", [128, T])
        headm = sb("headm", [KD, H])
        carry = sb("carry", [KD, 2, T])
        s0 = sb("s0", [128, D]); st6 = sb("st6", [128, 2, 6]); mv = sb("mv", [128, 2, 2])
        rs0 = sb("rs0", [128, 1]); rs1 = sb("rs1", [128, 1]); ve = sb("ve", [128, 2])
        xn0 = sb("xn0", [128, D]); xg = sb("xg", [128, D]); xn = sb("xn", [ROWS, D])
        hnT = sb("hnT", [DH, 2, 2, 64])
        zz = sb("zz", [KD, ROWS]); mz = sb("mz", [KD, ROWS]); az = sb("az", [KD, ROWS]); ez = sb("ez", [KD, ROWS])
        lz = sb("lz", [KD, ROWS]); gl = sb("gl", [KD, 2, T]); gs = sb("gs", [KD, 2, T])
        dd = sb("dd", [KD, 2, T]); dc = sb("dc", [KD, 2, T]); eq = sb("eq", [KD, ROWS]); ek = sb("ek", [KD, ROWS])
        qt = sb("qt", [KD, 2, T]); kt = sb("kt", [KD, 2, 2, 64]); qx = sb("qx", [KD, 2, 2, H, T])
        vv = sb("vv", [128, 2, H, 2, HV]); att = sb("att", [128, 2, H, T])
        lms = sb("lms", [T, H * 2]); rs_est = sb("rs_est", [T, H * 2]); rs_sq = sb("rs_sq", [T, H * 2])
        rs_xs = sb("rs_xs", [T, H * 2]); sq = sb("sq", [T, H * 2 * HV]); ms = sb("ms", [T, H * 2]); mse = sb("mse", [T, H * 2]); rso = sb("rso", [T, H * 2])
        on = sb("on", [T, 2, D]); eg = sb("eg", [DH, 2 * ROWS]); eln = sb("eln", [DH, 2 * ROWS])
        sg = sb("sg", [DH, 2 * ROWS]); oT = sb("oT", [DH, 2, 2, ROWS])

        ps_tok, ps_T, ps_qkg, ps_vg, ps_sa, ps_sb, ps_o, ps_wo = psum
        block = ctx.enter_context(nc.Block())

        N, DEPTH = PAIRS, 5
        T0 = 6

        def ticks(eng, body):
            for t in range(T0):
                body(t, t % 2, lambda d, t=t: 0 <= t - d < N, t)
            with eng.Fori(0, (N - 2 - T0) // 2) as j:
                for u in range(2):
                    body(T0 + u + 2 * j, u, lambda d: True, T0)
            for t in range(N - 2, N + DEPTH):
                body(t, t % 2, lambda d, t=t: 0 <= t - d < N, t)

        @block.sync
        def _(eng):
            eng.wait_ge(S("cleared"), 1)
            n = 0
            for s, (u0, v0) in enumerate(SH):
                for c in range(C):
                    wsrc = tok_W[(s * C + c) * PATCH * PATCH:(s * C + c + 1) * PATCH * PATCH, :].rearrange(
                        "(i j) e -> i j e", j=PATCH)
                    nlo = HALF - v0
                    p = c * WIN + u0
                    eng.dma_start(stage[p:p + PATCH, s, v0:HALF, :], wsrc[:, 0:nlo, :]).then_inc(S("w_in"), 16)
                    eng.dma_start(stage[KHI + p:KHI + p + PATCH, s, 0:PATCH - nlo, :],
                                  wsrc[:, nlo:PATCH, :]).then_inc(S("w_in"), 16)
                    n += 2
            assert n == 30

            xr = x.rearrange("b c (y u) w -> c u b y w", u=PATCH)

            def load_rows(i, u):
                for b in range(2):
                    src = xr[:, :, bass.ds(i * 2 + b, 1), :, :]
                    for c in range(C):
                        p = c * WIN
                        eng.dma_start(raw[p + 1:p + 17, u, b, :, 1:1 + HW], src[c, :, 0]).then_inc(S(f"rows{u}"), 16)
                    eng.dma_start(raw[0:KC:WIN, u, b, 1:GRID, 1:1 + HW],
                                  src[:, PATCH - 1, 0, 0:GRID - 1, :]).then_inc(S(f"rows{u}"), 16)
                    eng.dma_start(raw[WIN - 1:KC:WIN, u, b, 0:GRID - 1, 1:1 + HW],
                                  src[:, 0, 0, 1:GRID, :]).then_inc(S(f"rows{u}"), 16)

            eng.wait_ge(S("img_clear"), 1)
            load_rows(0, 0)
            load_rows(1, 1)
            eng.wait_ge(S("weff_done"), 1)
            eng.wait_ge(S("cst"), 9)

            total = SLOTS * D // 128 // ZW
            per = total // NCHUNK
            with eng.Fori(0, NCHUNK) as j:
                for u in range(2):
                    hold(eng, "img", 4 * j + 2 * u + 2, "sp")
                    load_rows(2 * j + 2 + u, u)
                    if u == 0:
                        for half in range(2):
                            eng.dma_start(know[0:DH, bass.ds(j * (KCH * 2 * R), KCH * 2 * R)].rearrange(
                                              "p (n k r) -> p n k r", k=2, r=R)[:, :, half, :],
                                          f_know[bass.ds(j * KCH, KCH), half * DH:(half + 1) * DH, :].rearrange("n p r -> p n r")
                                          ).then_inc(S("know_in"), 16)
                    else:
                        clear(eng, S, zeros, xs_d, j * per, per)
            clear(eng, S, zeros, xs_d, NCHUNK * per, total - NCHUNK * per)
            eng.wait_ge(S("h1"), N)
            h1v = h1_d.rearrange("(i b t) d -> b t i d", b=2, t=T)
            for b in range(2):
                eng.dma_start(h1v[b, 1:T], h_res[b * NPATCH:(b + 1) * NPATCH, :, :]).then_inc(S("h1_out"), 16)
                eng.dma_start(h1v[b, 0:1], h_res[PROWS + b:PROWS + b + 1, :, :]).then_inc(S("h1_out"), 16)
            eng.wait_ge(S("h1_out"), 64)
            eng.wait_ge(S("know_in"), 32 * NCHUNK)
            eng.wait_ge(S("zeroed"), 16 * NCHUNK + 16)

        @block.gpsimd
        def _(eng):
            eng.memset(know[:, 0:5 * HALF * D], 0.0).then_inc(S("cleared"), 1)
            eng.memset(zeros[:, :], 0.0).then_inc(S("cst"), 1)
            eng.memset(mhalf[:, :], -0.5).then_inc(S("cst"), 1)
            eng.memset(ident[:, :], 0.0).then_inc(S("cst"), 1)
            eng.memset(causal[:, :], 0.0).then_inc(S("cst"), 1)
            eng.memset(headm[:, :], 1.0).then_inc(S("cst"), 1)
            eng.memset(carry[:, :, :], 1.0).then_inc(S("cst"), 1)
            eng.memset(kt[:, :, :, :], 0.0).then_inc(S("cst"), 1)
            eng.memset(vv[:, :, :, :, :], 0.0).then_inc(S("cst"), 1)
            eng.memset(hnT[:, :, :, :], 0.0).then_inc(S("cst"), 1)
            eng.wait_ge(S("cst"), 9)
            done = 0

            def masked(tile, keep, fill, base, step, channel):
                nonlocal done
                if done:
                    eng.wait_ge(S("masks"), done)
                eng.affine_select(out=tile, in_=tile, compare_op=keep, fill=fill, base=base,
                                  pattern=[[step, tile.shape[1]]], channel_multiplier=channel).then_inc(S("masks"), 1)
                done += 1

            masked(ident[:, :], ALU.not_equal, 1.0, 0, -1, 1)
            masked(headm[:, :], ALU.is_ge, 0.0, 0, -HK, 1)
            masked(headm[:, :], ALU.is_ge, 0.0, HK - 1, HK, -1)
            for b in range(2):
                half = causal[64 * b:64 * b + 64, :]
                masked(half[:, 0:NPATCH], ALU.is_gt, 1.0, 0, -1, 1)
                masked(half, ALU.not_equal, 1.0, -NPATCH, 0, 1)
            eng.wait_ge(S("masks"), done)
            eng.memset(carry[:, :, 0:1], 0.0).then_inc(S("masks"), 1)
            eng.memset(carry[:, :, NPATCH:T], 0.0).then_inc(S("masks"), 1)
            eng.wait_ge(S("masks"), NMASK)

            def power(dst, src, n, name):
                eng.tensor_tensor(dst, src, mhalf[0:src.shape[0], 0:n], ALU.pow).then_inc(S(name), 1)

            def tick(t, u, has, first):
                if has(0):
                    eng.wait_ge(S("ve0"), t + 1)
                    power(rs0[0:PROWS, :], ve[0:PROWS, 0:1], 1, "rs0")
                    eng.wait_ge(S("ve1"), t + 1)
                    power(rs1[0:ROWS, :], ve[0:ROWS, 1:2], 1, "rs1")
                if has(1):
                    i = t - 1
                    eng.wait_ge(S("qt"), i + 1)
                    if first >= 3:
                        eng.wait_ge(S("scores"), i - 1)
                    for b in range(2):
                        eng.tensor_tensor(qx[:, 1 - u, b, :, :], qt[:, b, :].unsqueeze(1).to_broadcast([KD, H, T]),
                                          headm[:, :].unsqueeze(2).to_broadcast([KD, H, T]),
                                          ALU.mult).then_inc(S("qx"), 1)

            ticks(eng, tick)

        @block.scalar
        def _(eng):
            eng.add_instruction(mybir.InstLoadActFuncSet(name=nc.get_next_instruction_name(),
                                                         act_func_set_id=EXP_LN_SET, ins=[], outs=[]))
            rowv = lambda v: v.rearrange("(o n) -> o n", o=1)
            for dst, src in ((tokb, tok_b), (gam, tok_gamma), (bet, tok_beta)):
                eng.dma_start(dst[:, :], rowv(src).to_broadcast([128, D])).then_inc(S("ld"), 16)
            eng.dma_start(h_res[PROWS:ROWS, :, :],
                          cls_tok.rearrange("a b d -> a (b d)").unsqueeze(1).to_broadcast([2, PAIRS, D])).then_inc(S("ld"), 16)
            for dst, src in ((wq, Wq), (wk, Wk), (wv, Wv), (wg, Wg), (wo, Wo), (wgk1, Wgk1)):
                eng.dma_start(dst[:, :, :], src.rearrange("(k p) n -> p k n", p=DH)).then_inc(S("ld"), 16)
            eng.dma_start(wgk2[:, :], Wgk2).then_inc(S("ld"), 16)
            eng.dma_start(bgk[:, :], bgk2.rearrange("(p o) -> p o", o=1)).then_inc(S("ld"), 16)
            for h in range(KD // HV):
                eng.dma_start(onw[h * HV:(h + 1) * HV, :], o_norm_w.rearrange("(p o) -> p o", o=1)).then_inc(S("ld"), 16)

            def spread(i, u, half, reused):
                if half == 0:
                    hold(eng, f"rows{u}", 160 + (i // 2 * 160 if isinstance(i, int) else (i - u) * 80), "act")
                    if reused:
                        hold(eng, "tok", i - 1, "act")
                eng.activation(img[half * KHI:half * KHI + KC, u, :, :, 0:XW - HALF],
                               raw[:, u, :, :, half * HALF:half * HALF + XW - HALF], ACT.Copy).then_inc(S("img"), 1)

            eng.wait_ge(S("img_clear"), 2)
            for half in range(2):
                spread(0, 0, half, False)

            def tick(t, u, has, first):
                if has(1):
                    i = t - 1
                    eng.wait_ge(S("T1"), i + 1)
                    if first >= 2:
                        eng.wait_ge(S("proj"), i)
                    src = ps_T[0:DH, 0:2 * ROWS].rearrange("p (k c) -> p k c", k=2)
                    eng.activation(hnT[:, :, :, 0:NPATCH], src[:, :, 0:PROWS].rearrange("p k (b t) -> p k b t", b=2),
                                   ACT.Copy).then_inc(S("hnT"), 1)
                    eng.activation(hnT[:, :, :, NPATCH], src[:, :, PROWS:ROWS], ACT.Copy).then_inc(S("hnT"), 1)
                if has(-1):
                    spread(t + 1, 1 - u, 0, first >= 1)
                if has(1):
                    i = t - 1
                    gk = ps_qkg[0:KD, 2 * ROWS:3 * ROWS]
                    eng.wait_ge(S("gkps"), i + 1)
                    if first >= 2:
                        eng.wait_ge(S("mz"), i)
                    eng.activation(zz[:, :], gk, ACT.Identity, bias=bgk[:, 0:1]).then_inc(S("zz"), 1)
                    eng.wait_ge(S("zz"), i + 1)
                    eng.activation(az[:, :], zz[:, :], ACT.Abs).then_inc(S("az"), 1)
                    eng.wait_ge(S("az"), i + 1)
                    eng.activation(ez[:, :], az[:, :], ACT.Exp, scale=-1.0).then_inc(S("ez"), 1)
                    eng.wait_ge(S("ez"), i + 1)
                    if first >= 2:
                        eng.wait_ge(S("gl"), i)
                    eng.activation(lz[:, :], ez[:, :], ACT.Ln, bias=1.0).then_inc(S("lz"), 1)
                    eng.wait_ge(S("proj"), i + 1)
                    if first >= 2:
                        eng.wait_ge(S("eln"), i)
                    eng.activation(eg[:, :], ps_vg[0:DH, D:D + 2 * ROWS], ACT.Exp, scale=-1.0).then_inc(S("eg"), 1)
                if has(-1):
                    spread(t + 1, 1 - u, 1, first >= 1)
                if has(1):
                    i = t - 1
                    eng.wait_ge(S("eg"), i + 1)
                    eng.activation(eln[:, :], eg[:, :], ACT.Ln, bias=1.0).then_inc(S("eln"), 1)
                    if first >= 3:
                        eng.wait_ge(S("pv"), i - 1)
                    for b in range(2):
                        eng.activation(vv[64 * b:64 * b + 64, 1 - u, :, b, :],
                                       ps_vg[64 * b:64 * b + 64, 0:D].rearrange("p (h v) -> p h v", h=H),
                                       ACT.Copy).then_inc(S("vv"), 1)
                if has(3):
                    i = t - 3
                    eng.wait_ge(S("pv"), i + 1)
                    if first >= 4:
                        eng.wait_ge(S("ms"), i)
                    eng.activation(sq[:, :], ps_o[0:T, 0:2 * D], ACT.Square).then_inc(S("sq"), 1)
                if has(1):
                    i = t - 1
                    eng.wait_ge(S("eln"), i + 1)
                    if first >= 2:
                        eng.wait_ge(S("gate"), i)
                    eng.activation(sg[:, :], eln[:, :], ACT.Exp, scale=-1.0).then_inc(S("sg"), 1)
                    eng.wait_ge(S("dc"), i + 1)
                    if first >= 2:
                        eng.wait_ge(S("qt"), i)
                        eng.wait_ge(S("kt"), i)
                    flat = dc[:, :, :].rearrange("p b t -> p (b t)")
                    eng.activation(ek[:, :], flat, ACT.Exp, scale=-1.0 / GATE_DIV).then_inc(S("ek"), 1)
                    eng.activation(eq[:, :], flat, ACT.Exp, scale=1.0 / GATE_DIV).then_inc(S("eq"), 1)
                if has(3):
                    i = t - 3
                    eng.wait_ge(S("mse"), i + 1)
                    eng.activation(lms[:, :], mse[:, :], ACT.Ln).then_inc(S("lms"), 1)
                    eng.wait_ge(S("lms"), i + 1)
                    if first >= 4:
                        eng.wait_ge(S("rso"), i)
                    eng.activation(rs_est[:, :], lms[:, :], ACT.Exp, scale=-0.5).then_inc(S("rs_est"), 1)

            ticks(eng, tick)

        @block.vector
        def _(eng):
            eng.memset(raw[:, :, :, :, :], 0.0).then_inc(S("img_clear"), 1)
            eng.memset(img[32:KHI, :, :, :, :], 0.0).then_inc(S("img_clear"), 1)
            eng.wait_ge(S("w_in"), 480)
            for n in range(4):
                a = stage[0:KHI + KC, 0] if n == 0 else weff[:, :, :]
                if n:
                    eng.wait_ge(S("wsum"), n)
                eng.tensor_tensor(weff[:, :, :], a, stage[0:KHI + KC, n + 1], ALU.add).then_inc(S("wsum"), 1)
            eng.wait_ge(S("wsum"), 4)
            eng.wait_ge(S("ld"), 16 * 18)
            eng.wait_ge(S("masks"), NMASK)
            eng.tensor_scalar(wo[:, :, :], wo[:, :, :], onw[:, 0:1], None, ALU.mult).then_inc(S("weff_done"), 1)
            eng.wait_ge(S("wgkps"), 1)
            eng.tensor_copy(wgk1T[:, :, :], ps_T[0:LR, 0:D].rearrange("p (k c) -> p k c", k=2)).then_inc(S("wgk"), 1)
            eng.wait_ge(S("wgkps"), 2)
            eng.tensor_copy(wgk[:, :, :], ps_T[0:DH, 0:2 * KD].rearrange("p (k c) -> p k c", k=2)).then_inc(S("wgk"), 1)

            def bn(src, rows, l, i):
                eng.bn_stats(st6[0:rows, l, :], src).then_inc(S(f"st{l}"), 1)

            def aggregate(rows, l, i):
                hold(eng, f"st{l}", i + 1, "dve")
                eng.bn_aggr(mv[0:rows, l, :], st6[0:rows, l, :]).then_inc(S(f"mv{l}"), 1)

            def variance(rows, l, i):
                eng.wait_ge(S(f"mv{l}"), i + 1)
                eng.tensor_scalar(ve[0:rows, l:l + 1], mv[0:rows, l, 1:2], EPS, None, ALU.add).then_inc(S(f"ve{l}"), 1)

            def tick(t, u, has, first):
                new, gk, n, w = t, t - 1, t - 4, t - 5
                if has(0):
                    eng.wait_ge(S("tok"), new + 1)
                    eng.tensor_tensor(s0[0:PROWS, :], ps_tok[0:PROWS, 0:D], tokb[0:PROWS, :], ALU.add).then_inc(S("s0"), 1)
                if has(4):
                    eng.wait_ge(S("rs_est"), n + 1)
                    eng.tensor_tensor(rs_sq[:, :], rs_est[:, :], rs_est[:, :], ALU.mult).then_inc(S("newton"), 1)
                if has(0):
                    hold(eng, "s0", new + 1, "dve")
                    bn(s0[0:PROWS, :], PROWS, 0, new)
                if has(4):
                    eng.wait_ge(S("newton"), 2 * n + 1)
                    eng.scalar_tensor_tensor(out=rs_xs[:, :], in0=rs_sq[:, :], scalar=-0.5, in1=mse[:, :],
                                             op0=ALU.mult, op1=ALU.mult).then_inc(S("newton"), 1)
                if has(0):
                    aggregate(PROWS, 0, new)
                if has(4):
                    eng.wait_ge(S("newton"), 2 * n + 2)
                    eng.scalar_tensor_tensor(out=rso[:, :], in0=rs_xs[:, :], scalar=1.5, in1=rs_est[:, :],
                                             op0=ALU.add, op1=ALU.mult).then_inc(S("rso"), 1)
                if has(0):
                    variance(PROWS, 0, new)
                if has(4):
                    eng.wait_ge(S("rso"), n + 1)
                    if first >= 5:
                        eng.wait_ge(S("T2"), n)
                    eng.tensor_tensor(on[:, :, :].rearrange("p b (h v) -> p h b v", h=H),
                                      ps_o[0:T, 0:2 * D].rearrange("p (h b v) -> p h b v", h=H, b=2),
                                      rso[:, :].rearrange("p (h b) -> p h b", h=H).unsqueeze(3).to_broadcast([T, H, 2, HV]),
                                      ALU.mult).then_inc(S("on"), 1)
                if has(5):
                    eng.wait_ge(S("wo"), w + 1)
                    eng.tensor_tensor(h_res[0:ROWS, w, :], h_res[0:ROWS, w, :], ps_wo[0:ROWS, 0:D],
                                      ALU.add).then_inc(S("h1"), 1)
                if has(0):
                    eng.wait_ge(S("rs0"), new + 1)
                    eng.tensor_scalar(xn0[0:PROWS, :], s0[0:PROWS, :], mv[0:PROWS, 0, 0:1], rs0[0:PROWS, 0:1],
                                      ALU.subtract, ALU.mult).then_inc(S("xn0"), 1)
                if has(1):
                    eng.wait_ge(S("zz"), gk + 1)
                    eng.tensor_scalar(mz[:, :], zz[:, :], 0.0, None, ALU.min).then_inc(S("mz"), 1)
                if has(0):
                    eng.wait_ge(S("xn0"), new + 1)
                    eng.tensor_tensor(xg[0:PROWS, :], xn0[0:PROWS, :], gam[0:PROWS, :], ALU.mult).then_inc(S("xg"), 1)
                if has(1):
                    eng.wait_ge(S("mz"), gk + 1)
                    eng.wait_ge(S("lz"), gk + 1)
                    eng.tensor_tensor(gl[:, :, :].rearrange("p b t -> p (b t)"), mz[:, :], lz[:, :],
                                      ALU.subtract).then_inc(S("gl"), 1)
                if has(0):
                    eng.wait_ge(S("xg"), new + 1)
                    eng.tensor_tensor(h_res[0:PROWS, new, :], xg[0:PROWS, :], bet[0:PROWS, :], ALU.add).then_inc(S("h0"), 1)
                if has(1):
                    eng.wait_ge(S("gl"), gk + 1)
                    eng.tensor_tensor(gl[:, :, 0:1], gl[:, :, 0:1], gl[:, :, NPATCH:T], ALU.add).then_inc(S("gl2"), 1)
                if has(0):
                    hold(eng, "h0", new + 1, "dve")
                    bn(h_res[0:ROWS, new, :], ROWS, 1, new)
                if has(1):
                    eng.wait_ge(S("gl2"), gk + 1)
                    eng.tensor_tensor_scan(gs[:, :, :].rearrange("p b t -> p (b t)"),
                                           carry[:, :, :].rearrange("p b t -> p (b t)"),
                                           gl[:, :, :].rearrange("p b t -> p (b t)"), 0.0, ALU.mult,
                                           ALU.add).then_inc(S("gs"), 1)
                if has(0):
                    aggregate(ROWS, 1, new)
                if has(1):
                    eng.wait_ge(S("gs"), gk + 1)
                    eng.tensor_tensor(dd[:, :, :], gs[:, :, :], gs[:, :, T // 2 - 1:T // 2].to_broadcast([KD, 2, T]),
                                      ALU.subtract).then_inc(S("dd"), 1)
                if has(0):
                    variance(ROWS, 1, new)
                if has(1):
                    eng.wait_ge(S("dd"), gk + 1)
                    if first >= 2:
                        eng.wait_ge(S("eq"), gk)
                    eng.tensor_scalar(dc[:, :, :], dd[:, :, :], -CLAMP, CLAMP, ALU.max, ALU.min).then_inc(S("dc"), 1)
                if has(3):
                    i = t - 3
                    eng.wait_ge(S("sq"), i + 1)
                    eng.tensor_reduce(ms[:, :], sq[:, :].rearrange("p (g v) -> p g v", v=HV), AX.X,
                                      ALU.add).then_inc(S("ms"), 1)
                if has(0):
                    eng.wait_ge(S("rs1"), new + 1)
                    if first >= 1:
                        eng.wait_ge(S("T1"), new)
                    eng.tensor_scalar(xn[:, :], h_res[0:ROWS, new, :], mv[0:ROWS, 1, 0:1], rs1[0:ROWS, 0:1],
                                      ALU.subtract, ALU.mult).then_inc(S("xn"), 1)
                if has(3):
                    i = t - 3
                    eng.wait_ge(S("ms"), i + 1)
                    if first >= 4:
                        eng.wait_ge(S("newton"), 2 * i)
                        eng.wait_ge(S("lms"), i)
                    eng.tensor_scalar(mse[:, :], ms[:, :], 1.0 / HV, EPS, ALU.mult, ALU.add).then_inc(S("mse"), 1)
                if has(1):
                    i = t - 1
                    eng.wait_ge(S("ek"), i + 1)
                    if first >= 3:
                        eng.wait_ge(S("scores"), i - 1)
                    eng.tensor_tensor(kt[:, 1 - u, :, 0:T], ps_qkg[0:KD, ROWS:2 * ROWS].rearrange("p (b t) -> p b t", b=2),
                                      ek[:, :].rearrange("p (b t) -> p b t", b=2), ALU.mult).then_inc(S("kt"), 1)
                    eng.wait_ge(S("eq"), i + 1)
                    if first >= 2:
                        eng.wait_ge(S("qx"), 2 * i)
                    eng.scalar_tensor_tensor(out=qt[:, :, :], in0=ps_qkg[0:KD, 0:ROWS].rearrange("p (b t) -> p b t", b=2),
                                             scalar=float(HK) ** -0.5, in1=eq[:, :].rearrange("p (b t) -> p b t", b=2),
                                             op0=ALU.mult, op1=ALU.mult).then_inc(S("qt"), 1)
                if has(4):
                    i = t - 4
                    eng.wait_ge(S("T2"), i + 1)
                    if first >= 6:
                        eng.wait_ge(S("wo"), i - 1)
                    src = ps_T[0:DH, 256:256 + 2 * ROWS].rearrange("p (k b t) -> p k b t", k=2, b=2)
                    gv = gate[:, bass.ds(i, 1), :, :].rearrange("p o k (b t) -> p (o k) b t", b=2)
                    dst = oT[:, u, :, :]
                    eng.tensor_tensor(dst[:, :, 0:PROWS].rearrange("p k (b t) -> p k b t", b=2), src[:, :, :, 0:NPATCH],
                                      gv[:, :, :, 0:NPATCH], ALU.mult).then_inc(S("oT"), 1)
                    eng.tensor_tensor(dst[:, :, PROWS:ROWS], src[:, :, :, NPATCH], gv[:, :, :, NPATCH],
                                      ALU.mult).then_inc(S("oT"), 1)
                if has(1):
                    i = t - 1
                    eng.wait_ge(S("sg"), i + 1)
                    eng.wait_ge(S("vv"), 2 * i + 2)
                    eng.tensor_tensor(gate[:, bass.ds(i, 1), :, :].rearrange("p o k c -> p (o k) c"), ps_vg[0:DH, D:D + 2 * ROWS].rearrange("p (k c) -> p k c", k=2),
                                      sg[:, :].rearrange("p (k c) -> p k c", k=2), ALU.mult).then_inc(S("gate"), 1)
                if has(2):
                    i = t - 2
                    if first >= 4:
                        eng.wait_ge(S("pv"), i - 1)
                    eng.wait_ge(S("scores"), i + 1)
                    for n, bank in enumerate((ps_sa, ps_sb)):
                        eng.tensor_tensor(att[:, u, 6 * n:6 * n + 6, :],
                                          bank[:, 0:300].rearrange("p (h t) -> p h t", h=6),
                                          causal[:, :].unsqueeze(1).to_broadcast([128, 6, T]),
                                          ALU.mult).then_inc(S("att"), 1)
            ticks(eng, tick)

        @block.tensor
        def _(eng):
            eng.wait_ge(S("weff_done"), 1)
            for k in range(2):
                last = eng.transpose(ps_T[0:LR, k * DH:(k + 1) * DH], wgk1[:, k, :], ident[0:DH, 0:DH])
            last.then_inc(S("wgkps"), 1)
            eng.wait_ge(S("wgk"), 1)
            for k in range(2):
                last = eng.matmul(ps_T[0:DH, k * KD:(k + 1) * KD], wgk1T[:, k, :], wgk2[:, :], start=True, stop=True)
            last.then_inc(S("wgkps"), 1)
            eng.wait_ge(S("wgk"), 2)

            def tick(t, u, has, first):
                if has(0):
                    i = t
                    eng.wait_ge(S("img"), 2 * i + 2)
                    if first >= 1:
                        eng.wait_ge(S("s0"), i)
                    for v in range(HALF):
                        lhs = img[:, u, :, :, :].rearrange("p b y w -> p (b y w)")[:, v:v + PATCH * (PROWS - 1) + 1:PATCH]
                        last = eng.matmul(ps_tok[0:PROWS, 0:D], lhs, weff[:, v, :], start=(v == 0), stop=(v == HALF - 1))
                    last.then_inc(S("tok"), 1)
                if has(1):
                    i = t - 1
                    if first >= 5:
                        hold(eng, "oT", 2 * (i - 3), "pe")
                    eng.wait_ge(S("xn"), i + 1)
                    if first >= 2:
                        eng.wait_ge(S("hnT"), 2 * i)
                    for k in range(2):
                        last = eng.transpose(ps_T[0:DH, k * ROWS:(k + 1) * ROWS], xn[:, k * DH:(k + 1) * DH],
                                             ident[0:ROWS, 0:ROWS])
                    last.then_inc(S("T1"), 1)
                if has(5):
                    i = t - 5
                    eng.wait_ge(S("oT"), 2 * i + 2)
                    if first >= 6:
                        eng.wait_ge(S("h1"), i)
                    for k in range(2):
                        last = eng.matmul(ps_wo[0:ROWS, 0:D], oT[:, 1 - u, k, :], wo[:, k, :], start=(k == 0), stop=(k == 1))
                    last.then_inc(S("wo"), 1)

                if has(1):
                    i = t - 1
                    eng.wait_ge(S("hnT"), 2 * i + 2)
                    if first >= 2:
                        eng.wait_ge(S("qt"), i)
                        eng.wait_ge(S("kt"), i)
                    for slot, w in ((2, wgk), (1, wk), (0, wq)):
                        for k in range(2):
                            last = eng.matmul(ps_qkg[0:KD, slot * ROWS:(slot + 1) * ROWS], w[:, k, :], hnT[:, k, :, 0:T],
                                              start=(k == 0), stop=(k == 1))
                    last.then_inc(S("gkps"), 1)
                    if first >= 2:
                        eng.wait_ge(S("gate"), i)
                        eng.wait_ge(S("vv"), 2 * i)
                    for m in range(2):
                        for k in range(2):
                            eng.matmul(ps_vg[0:DH, D + m * ROWS:D + (m + 1) * ROWS], wg[:, k, m * DH:(m + 1) * DH],
                                       hnT[:, k, :, 0:T], start=(k == 0), stop=(k == 1))
                    for k in range(2):
                        last = eng.matmul(ps_vg[:, 0:D], hnT[:, k, :, :], wv[:, k, :], start=(k == 0), stop=(k == 1))
                    last.then_inc(S("proj"), 1)
                if has(3):
                    i = t - 3
                    eng.wait_ge(S("att"), 2 * i + 2)
                    eng.wait_ge(S("vv"), 2 * i + 2)
                    if first >= 4:
                        eng.wait_ge(S("on"), i)
                    for h in range(H):
                        last = eng.matmul(ps_o[0:T, h * 2 * HV:(h + 1) * 2 * HV], att[:, 1 - u, h, :],
                                          vv[:, 1 - u, h, :, :], start=True, stop=True)
                    last.then_inc(S("pv"), 1)
                if has(4):
                    i = t - 4
                    hold(eng, "on", i + 1, "pe")
                    if first >= 5:
                        hold(eng, "oT", 2 * i, "pe")
                    for b in range(2):
                        for k in range(2):
                            c = 256 + k * ROWS + b * T
                            last = eng.transpose(ps_T[0:DH, c:c + T], on[:, b, k * DH:(k + 1) * DH], ident[0:T, 0:T])
                    last.then_inc(S("T2"), 1)
                if has(2):
                    i = t - 2
                    eng.wait_ge(S("qx"), 2 * i + 2)
                    eng.wait_ge(S("kt"), i + 1)
                    if first >= 3:
                        eng.wait_ge(S("att"), 2 * i)
                    for b in range(2):
                        for n, bank in enumerate((ps_sa, ps_sb)):
                            last = eng.matmul(bank[64 * b:64 * b + 64, 0:300], kt[:, u, b, :],
                                              qx[:, u, b, 6 * n:6 * n + 6, :], start=True, stop=True)
                    last.then_inc(S("scores"), 1)
            ticks(eng, tick)


def part2(K, f_know, r_know, W_fk, b_fk, W_rk, b_rk, emb_fk, emb_rk):
    nc, S, hold, know, ident, mhalf, psum, zeros = (
        K[k] for k in ("nc", "S", "hold", "know", "ident", "mhalf", "psum", "zeros"))
    h1_d, out_d = K["h1_d"], K["out_d"]
    sorted_in = (K["xs_d"], K["hs_d"])
    sorted_out = (K["hp_d"], K["op_d"])
    width_in, width_out = (D, R), (R, D)
    NT4 = NG * GQ
    HT = NT4 // 2
    IDX, EXPS, ZS, REC = 0, 8, 16, 18

    with ExitStack() as ctx:
        def sb(name, shape, dt=F32):
            return ctx.enter_context(nc.sbuf_tensor(name, shape, dt))

        h1c = sb("h1c", [128, NTILE, D]); hn2 = sb("hn2", [128, NTILE, D])
        rank = sb("rank", [128, NTILE, 2 * NN], U16)
        rec = sb("rec", [128, REC]); recs = sb("recs", [128, NTILE, REC])
        wcat = sb("wcat", [DH, 2, 2 * DS]); bcat = sb("bcat", [2 * DS, 1])
        emb = sb("emb", [128, 2, 2 * DS]); embT = sb("embT", [2 * DS, 2, NN])
        esq = sb("esq", [128, DS]); ess = sb("ess", [128, 2]); enr = sb("enr", [128, 2]); einv = sb("einv", [128, 2])
        phalf = sb("phalf", [128, 2])
        colI = sb("colI", [128, NN], I32); col = sb("col", [128, NN]); colb = sb("colb", [128, NN], BF16)
        rowI = sb("rowI", [128, 2], I32); row = sb("row", [128, 2])
        before = sb("before", [128, 128], BF16)
        upto = sb("upto", [128, 128], BF16)
        onesf = sb("onesf", [128, NN])
        st6 = sb("st6b", [128, 6]); mv = sb("mvb", [128, 2]); ve = sb("veb", [128, 1]); rs = sb("rsb", [128, 1])
        xn2 = sb("xn2", [128, D]); hT2 = sb("hT2", [DH, 2, 128]); qT = sb("qT", [2 * DS, 128])
        lg = sb("lg", [128, 2, NN]); m8 = sb("m8", [128, 2, 8]); i8 = sb("i8", [128, 2, 8], U32)
        negm = sb("negm", [128, 2]); junk = sb("junk", [128, NN])
        oh = sb("oh", [128, TOPK, 2, NN], BF16)
        se = sb("se", [128, NTILE, 2]); zs = sb("zs", [128, NTILE, 2]); rw = sb("rw", [128, NTILE, 2])
        wts = sb("wts", [128, NTILE, 2, TOPK])
        cI = sb("cI", [128, 2, NN], I32); cS = sb("cS", [128, 2, NN], I32); ntl = sb("ntl", [128, 2, NN])
        incl = sb("incl", [128, 2, NN]); off0 = sb("off0", [128, 2, NN]); off = sb("off", [128, 2, NN])
        eidc = sb("eidc", [128, 2, 2]); eid = sb("eid", [1, 2, NT4], I32)
        ro = sb("ro", [128, NN]); pj = sb("pj", [128, NN]); posf = sb("posf", [128, TOPK])
        posI = sb("posI", [128, 2, 2, TOPK], I32); pos_all = sb("pos_all", [128, NTILE, 2, TOPK], I32)
        gposI = sb("gposI", [128, 2, TOPK], I32)
        rows_out = sb("rows_out", [128, 2, D])
        pjs = sb("pjs", [128, TOPK, NN])
        block = ctx.enter_context(nc.Block())

        N, T0 = NTILE, 5

        def ticks(eng, body, depth, n=N, t0=T0):
            for t in range(t0):
                body(t, t % 2, lambda d, t=t: 0 <= t - d < n, t)
            with eng.Fori(0, (n - t0) // 2) as j:
                for u in range(2):
                    body(t0 + u + 2 * j, (t0 + u) % 2, lambda d: True, t0)
            for t in range(n, n + depth):
                body(t, t % 2, lambda d, t=t: 0 <= t - d < n, t)

        G0 = 4
        free = hn2[:, :, :].rearrange("p n d -> p (n d)")
        spare = lambda n: free[:, n * 2 * GQ * D:(n + 1) * 2 * GQ * D].rearrange("p (u q d) -> p u q d", u=2, d=D)
        xg, eo, got = spare(0), spare(1), spare(2)
        free1 = h1c[:, :, :].rearrange("p n d -> p (n d)")
        xT = free1[:, 0:2 * GQ * 256].rearrange("p (u c) -> p u c", u=2)
        at = 2 * GQ * 256
        acc = free1[:, at:at + TOPK * D].rearrange("p (j d) -> p j d", d=D)
        at += TOPK * D
        resid = free1[:, at:at + 2 * D].rearrange("p (u d) -> p u d", d=D)

        def group_rows(dram, g):
            return dram[bass.ds(g * (GQ * 128), GQ * 128), :].rearrange("(q p) d -> p q d", p=128)

        def xg_of(r, u):
            return xg[:, u, :, :].rearrange("p q d -> p (q d)")[:, 0:GQ * width_in[r]].rearrange(
                "p (q d) -> p q d", q=GQ)

        def eo_of(r, u):
            return eo[:, u, :, :].rearrange("p q d -> p (q d)")[:, 0:GQ * width_out[r]].rearrange(
                "p (q d) -> p q d", q=GQ)

        @block.sync
        def _(eng):
            eng.dma_start(h1c[:, :, :], h1_d.rearrange("(n p) d -> p n d", p=128)).then_inc(S("h1c"), 16)
            for half in range(2):
                eng.dma_start(know[0:DH, TAIL * 2 * R:].rearrange("p (n k r) -> p n k r", k=2, r=R)[:, :, half, :],
                              f_know[TAIL:NN, half * DH:(half + 1) * DH, :].rearrange("n p r -> p n r")
                              ).then_inc(S("know2"), 16)
            total = SLOTS * R // 128 // ZW
            for c in range(4):
                clear(eng, S, zeros, K["hs_d"], c * (total // 4), total // 4)

            for r in range(2):
                for u in range(2):
                    eng.wait_ge(S(f"scat{r}{u}"), 64 * ((N + 1 - u) // 2))

                def tick(t, u, has, first, r=r):
                    if has(0):
                        if first >= 2:
                            hold(eng, f"xTp{r}", t - 1, "sp")
                        eng.dma_start(xg_of(r, u), group_rows(sorted_in[r], t)).then_inc(S(f"rows_in{r}{u}"), 16)

                ticks(eng, tick, 0, NG, G0)
                if r == 0:
                    eng.wait_ge(S("prod0"), NG)
                    for c in range(4):
                        n0 = c * (NN // 4)
                        eng.dma_start(know[:, n0 * D:(n0 + NN // 4) * D].rearrange("p (n d) -> p n d", d=D),
                                      r_know[n0:n0 + NN // 4].rearrange("n r d -> r n d")).then_inc(S("rknow"), 16)

            def tick(t, u, has, first):
                if has(0):
                    if first >= 2:
                        hold(eng, "y", t - 1, "sp")
                    eng.dma_start(resid[:, u, :], h1_d[bass.ds(t * 128, 128), :]).then_inc(S(f"resid{u}"), 16)
                if has(1):
                    i = t - 1
                    hold(eng, "y", i + 1, "sp")
                    eng.dma_start(out_d[bass.ds(i * 128, 128), :], rows_out[:, 1 - u, :]).then_inc(S(f"out{1 - u}"), 16)

            ticks(eng, tick, 1)
            for u in range(2):
                eng.wait_ge(S(f"out{u}"), 16 * ((N + 1 - u) // 2))

        @block.gpsimd
        def _(eng):
            eng.memset(emb[:, :, :], 0.0).then_inc(S("emb0"), 1)
            eng.memset(phalf[:, :], 0.5).then_inc(S("cst2"), 1)
            eng.memset(onesf[:, :], 1.0).then_inc(S("cst2"), 1)
            eng.memset(before[:, :], 1.0).then_inc(S("cst2"), 1)
            eng.memset(upto[:, :], 1.0).then_inc(S("cst2"), 1)
            eng.iota(colI[:, :], pattern=[[1, NN]], base=0, channel_multiplier=0).then_inc(S("cst2"), 1)
            eng.iota(rowI[:, :], pattern=[[HT, 2]], base=0, channel_multiplier=1).then_inc(S("cst2"), 1)
            eng.wait_ge(S("cst2"), 6)
            eng.affine_select(out=before[:, :], in_=before[:, :], compare_op=ALU.is_gt, fill=0.0, base=0,
                              pattern=[[1, 128]], channel_multiplier=-1).then_inc(S("cst2"), 1)
            eng.wait_ge(S("cst2"), 7)
            eng.affine_select(out=upto[:, :], in_=upto[:, :], compare_op=ALU.is_ge, fill=0.0, base=0,
                              pattern=[[-1, 128]], channel_multiplier=1).then_inc(S("cst2"), 1)
            eng.wait_ge(S("cst2"), 8)
            eng.wait_ge(S("ess"), 2)
            eng.tensor_tensor(enr[:, :], ess[:, :], phalf[:, :], ALU.pow).then_inc(S("enr"), 1)

            def tick(t, u, has, first):
                if has(0):
                    eng.wait_ge(S("veb"), t + 1)
                    eng.tensor_tensor(rs[:, :], ve[:, :], mhalf[:, 0:1], ALU.pow).then_inc(S("rsb"), 1)

            ticks(eng, tick, 2)

            eng.wait_ge(S("ordered"), 1)

            def scatter(r, u, n_pos, n_rows, row_sem, dram, width):
                hold(eng, f"pos{r}", n_pos, "pool")
                hold(eng, row_sem, n_rows, "pool")
                for j in range(TOPK):
                    eng.indirect_dma_start(
                        out=dram, out_offset=bass.IndirectOffsetOnAxis(ap=posI[:, r, u, j:j + 1], axis=0),
                        in_=rows_out[:, u, 0:width], in_offset=None).then_inc(S(f"scat{r}{u}"), 16)

            def gather(u, dram, width, sem):
                for j in range(TOPK):
                    eng.indirect_dma_start(
                        out=got[:, u, j, 0:width], out_offset=None, in_=dram,
                        in_offset=bass.IndirectOffsetOnAxis(ap=gposI[:, u, j:j + 1], axis=0)).then_inc(S(f"{sem}{u}"), 16)

            def tick(t, u, has, first):
                if has(0):
                    scatter(0, u, t + 1, t + 1, "staged", sorted_in[0], D)

            ticks(eng, tick, 0)

            eng.wait_ge(S("zeroed"), 16 * (NCHUNK + 1 + 4))
            for u in range(2):
                eng.wait_ge(S(f"rows_out0{u}"), 16 * (NG // 2))

            def tick(t, u, has, first):
                if has(0):
                    hold(eng, "gpos", t + 1, "pool")
                    if first >= 2:
                        hold(eng, "mix", 4 * (t - 1), "pool")
                    gather(u, sorted_out[0], R, "gath")
                if has(1):
                    scatter(1, 1 - u, t, 4 * t, "mix", sorted_in[1], R)

            ticks(eng, tick, 1)
            for u in range(2):
                eng.wait_ge(S(f"rows_out1{u}"), 16 * (NG // 2))

            def tick(t, u, has, first):
                if has(0):
                    hold(eng, "gpos", N + t + 1, "pool")
                    if first >= 2:
                        hold(eng, "y", t - 1, "pool")
                    gather(u, sorted_out[1], D, "gathy")

            ticks(eng, tick, 0)

        @block.scalar
        def _(eng):
            eng.wait_ge(S("emb0"), 1)
            for r, (W, bias, e) in enumerate(((W_fk, b_fk, emb_fk), (W_rk, b_rk, emb_rk))):
                cols = slice(r * DS, (r + 1) * DS)
                eng.dma_start(wcat[:, :, cols], W.rearrange("(k p) n -> p k n", p=DH)).then_inc(S("ld2"), 16)
                eng.dma_start(bcat[cols, :], bias.rearrange("(p o) -> p o", o=1)).then_inc(S("ld2"), 16)
                eng.dma_start(emb[:, r, cols], e).then_inc(S("ld2"), 16)
            eng.wait_ge(S("ld2"), 96)
            for r in range(2):
                if r:
                    eng.wait_ge(S("ess"), 1)
                eng.activation(esq[:, :], emb[:, r, r * DS:(r + 1) * DS], ACT.Square,
                               accum_out=ess[:, r:r + 1]).then_inc(S("ess"), 1)
            eng.wait_ge(S("embTp"), 1)
            eng.activation(embT[:, :, :], psum[4][:, 0:2 * NN].rearrange("p (r n) -> p r n", r=2),
                           ACT.Copy).then_inc(S("embT"), 1)

            def tick(t, u, has, first):
                if has(4):
                    i = t - 4
                    eng.wait_ge(S("rankp"), i + 1)
                    eng.activation(rank[:, i, :], psum[0][:, 0:2 * NN], ACT.Copy).then_inc(S("rank"), 1)
                if has(1):
                    i = t - 1
                    eng.wait_ge(S("T3"), i + 1)
                    if first >= 2:
                        eng.wait_ge(S("qp"), i)
                    eng.activation(hT2[:, :, :], psum[2][0:DH, 0:256].rearrange("p (k c) -> p k c", k=2),
                                   ACT.Copy).then_inc(S("hT2"), 1)
                    eng.activation(hn2[:, i, :], xn2[:, :], ACT.Copy).then_inc(S("hn2"), 1)
                if has(3):
                    i = t - 3
                    eng.wait_ge(S("negm"), i + 1)
                    if first >= 4:
                        eng.wait_ge(S("recs"), i)
                    for r in range(2):
                        if r or first >= 4:
                            eng.wait_ge(S("esum"), 2 * i + r)
                        eng.activation(junk[:, :], lg[:, r, :], ACT.Exp, bias=negm[:, r:r + 1],
                                       accum_out=rec[:, ZS + r:ZS + r + 1]).then_inc(S("esum"), 1)
                    for r in range(2):
                        eng.activation(rec[:, EXPS + 4 * r:EXPS + 4 * r + 4], m8[:, r, 0:TOPK], ACT.Exp,
                                       bias=negm[:, r:r + 1]).then_inc(S("e4"), 1)
                if has(2):
                    i = t - 2
                    eng.wait_ge(S("lgp"), i + 1)
                    if first >= 3:
                        eng.wait_ge(S("idx"), 2 * i)
                        eng.wait_ge(S("esum"), 2 * i)
                    eng.activation(lg[:, :, :], psum[1][:, 0:2 * NN].rearrange("p (r n) -> p r n", r=2),
                                   ACT.Copy).then_inc(S("lg"), 1)
                if has(1):
                    i = t - 1
                    eng.wait_ge(S("qp"), i + 1)
                    if first >= 2:
                        eng.wait_ge(S("lgp"), i)
                    eng.activation(qT[:, :], psum[3][:, 0:128], ACT.Identity, bias=bcat[:, 0:1]).then_inc(S("qT"), 1)

            ticks(eng, tick, 4)

            def tick(t, u, has, first):
                if has(0):
                    if first >= 2:
                        eng.wait_ge(S(f"scat0{u}"), 64 * (t // 2) if isinstance(t, int) else (t - u) * 32)
                    eng.activation(rows_out[:, u, :], hn2[:, t, :], ACT.Copy).then_inc(S("staged"), 1)

            ticks(eng, tick, 0)

            for r in range(2):
                def tick(t, u, has, first, r=r):
                    if has(0):
                        eng.wait_ge(S(f"xTp{r}"), t + 1)
                        if first >= 2:
                            eng.wait_ge(S(f"prod{r}"), t - 1)
                        eng.activation(xT[0:DH if r == 0 else 128, u, 0:512 if r == 0 else 256],
                                       psum[0][0:DH if r == 0 else 128, 0:512 if r == 0 else 256],
                                       ACT.Copy).then_inc(S(f"xTA{r}"), 1)
                    if has(1):
                        g = t - 1
                        eng.wait_ge(S(f"prod{r}"), g + 1)
                        if first >= 3:
                            eng.wait_ge(S(f"rows_out{r}{1 - u}"), (g // 2) * 16 if isinstance(g, int) else (g - 1 + u) * 8)
                        eng.activation(eo_of(r, 1 - u)[:, 0:2, :],
                                       psum[2 + 2 * (1 - u)][:, 0:2 * width_out[r]].rearrange("p (q d) -> p q d", q=2),
                                       ACT.Copy).then_inc(S(f"eoA{r}"), 1)
                        hold(eng, f"eoA{r}", g + 1, "act")
                        hold(eng, f"eoV{r}", g + 1, "act")
                        eng.dma_start(group_rows(sorted_out[r], g), eo_of(r, 1 - u)).then_inc(S(f"rows_out{r}{1 - u}"), 16)

                ticks(eng, tick, 1, NG, G0)

        @block.vector
        def _(eng):
            eng.wait_ge(S("cst2"), 8)
            eng.tensor_copy(col[:, :], colI[:, :]).then_inc(S("cst3"), 1)
            eng.tensor_copy(colb[:, :], colI[:, :]).then_inc(S("cst3"), 1)
            eng.tensor_copy(row[:, :], rowI[:, :]).then_inc(S("cst3"), 1)
            eng.wait_ge(S("enr"), 1)
            eng.tensor_scalar(einv[:, :], enr[:, :], 1e-8, None, ALU.add).then_inc(S("einv"), 1)
            eng.wait_ge(S("einv"), 1)
            eng.reciprocal(enr[:, :], einv[:, :]).then_inc(S("einv"), 1)
            eng.wait_ge(S("einv"), 2)
            for r in range(2):
                eng.tensor_scalar(emb[:, r, :], emb[:, r, :], enr[:, r:r + 1], None, ALU.mult).then_inc(S("einv"), 1)
            eng.wait_ge(S("cst3"), 3)
            eng.wait_ge(S("h1c"), 16)

            def tick(t, u, has, first):
                i = t - 3
                if has(0):
                    eng.bn_stats(st6[:, :], h1c[:, t, :]).then_inc(S("stb"), 1)
                if has(3):
                    hold(eng, "lg", i + 1, "dve")
                    if first >= 4:
                        hold(eng, "e4", 2 * i, "dve")
                    for r in range(2):
                        eng.max(m8[:, r, :], lg[:, r, :]).then_inc(S("m8"), 1)
                if has(0):
                    hold(eng, "stb", t + 1, "dve")
                    eng.bn_aggr(mv[:, :], st6[:, :]).then_inc(S("mvb"), 1)
                if has(3):
                    eng.wait_ge(S("m8"), 2 * i + 2)
                    eng.tensor_scalar(negm[:, :], m8[:, :, 0], -1.0, None, ALU.mult).then_inc(S("negm"), 1)
                if has(0):
                    eng.wait_ge(S("mvb"), t + 1)
                    eng.tensor_scalar(ve[:, :], mv[:, 1:2], EPS, None, ALU.add).then_inc(S("veb"), 1)
                if has(3):
                    for r in range(2):
                        eng.max_index(i8[:, r, :], m8[:, r, :], lg[:, r, :]).then_inc(S("idx"), 1)
                    eng.wait_ge(S("idx"), 2 * i + 2)
                    if first >= 4:
                        eng.wait_ge(S("recs"), i)
                    eng.tensor_copy(rec[:, IDX:IDX + 8].rearrange("p (r j) -> p r j", r=2),
                                    i8[:, :, 0:TOPK]).then_inc(S("recx"), 1)
                if has(0):
                    eng.wait_ge(S("rsb"), t + 1)
                    if first >= 1:
                        eng.wait_ge(S("hn2"), t)
                        eng.wait_ge(S("T3"), t)
                    eng.tensor_scalar(xn2[:, :], h1c[:, t, :], mv[:, 0:1], rs[:, 0:1], ALU.subtract,
                                      ALU.mult).then_inc(S("xn2"), 1)
                if has(3):
                    eng.wait_ge(S("recx"), i + 1)
                    if first >= 4:
                        eng.wait_ge(S("ranku"), i)
                    for r in range(2):
                        for j in range(TOPK):
                            eng.tensor_scalar(oh[:, j, r, :], colb[:, :], rec[:, IDX + 4 * r + j:IDX + 4 * r + j + 1],
                                              None, ALU.is_equal).then_inc(S("oh"), 1)
                    eng.wait_ge(S("e4"), 2 * i + 2)
                    eng.tensor_copy(recs[:, i, :], rec[:, :]).then_inc(S("recs"), 1)

            ticks(eng, tick, 4)

            eng.wait_ge(S("recs"), N)
            e_all = recs[:, :, EXPS:EXPS + 8].rearrange("p n (r j) -> p n r j", r=2)
            eng.tensor_reduce(se[:, :, :], e_all, AX.X, ALU.add).then_inc(S("w"), 1)
            eng.wait_ge(S("w"), 1)
            eng.scalar_tensor_tensor(out=zs[:, :, :], in0=recs[:, :, ZS:REC], scalar=1e-8, in1=se[:, :, :],
                                     op0=ALU.mult, op1=ALU.add).then_inc(S("w"), 1)
            eng.wait_ge(S("w"), 2)
            eng.reciprocal(rw[:, :, :], zs[:, :, :]).then_inc(S("w"), 1)
            eng.wait_ge(S("w"), 3)
            for r in range(2):
                eng.tensor_tensor(wts[:, :, r, :], e_all[:, :, r, :],
                                  rw[:, :, r:r + 1].to_broadcast([128, N, TOPK]), ALU.mult).then_inc(S("w"), 1)
            eng.wait_ge(S("ranku"), N)
            eng.wait_ge(S("rank"), N)
            eng.tensor_scalar(cI[:, :, :], psum[0][:, 0:2 * NN].rearrange("p (r n) -> p r n", r=2), 127.0, None,
                              ALU.add).then_inc(S("ord"), 1)
            eng.wait_ge(S("ord"), 1)
            eng.tensor_scalar(cS[:, :, :], cI[:, :, :], 7, None, ALU.logical_shift_right).then_inc(S("ord"), 1)
            eng.wait_ge(S("ord"), 2)
            eng.tensor_copy(ntl[:, :, :], cS[:, :, :]).then_inc(S("ord"), 1)
            eng.wait_ge(S("ord"), 3)
            for r in range(2):
                eng.tensor_tensor_scan(incl[:, r, :], onesf[:, :], ntl[:, r, :], 0.0, ALU.mult,
                                       ALU.add).then_inc(S("ord"), 1)
            eng.wait_ge(S("ord"), 5)
            eng.tensor_tensor(off0[:, :, :], incl[:, :, :], ntl[:, :, :], ALU.subtract).then_inc(S("ord"), 1)
            eng.wait_ge(S("ord"), 6)
            eng.tensor_scalar(off[:, :, :], off0[:, :, :], 128.0, None, ALU.mult).then_inc(S("ord"), 1)
            n = 7
            for r in range(2):
                for hh in range(2):
                    eng.wait_ge(S("ord"), n)
                    eng.scalar_tensor_tensor(out=pj[0:HT, :], in0=incl[0:HT, r, :], scalar=row[0:HT, hh:hh + 1],
                                             in1=onesf[0:HT, :], op0=ALU.is_le, op1=ALU.mult,
                                             accum_out=eidc[0:HT, r, hh:hh + 1]).then_inc(S("ord"), 1)
                    n += 1
            eng.wait_ge(S("ord"), n)
            eng.wait_ge(S("eidp"), 1)
            eng.tensor_scalar(eid[:, :, :], psum[1][0:1, 0:2 * NT4].rearrange("p (r n) -> p r n", r=2),
                              float(NN - 1), None, ALU.min).then_inc(S("ordered"), 1)
            eng.wait_ge(S("w"), 5)

            def positions(r, i, u, i_done):
                eng.wait_ge(S("ro"), N * r + i_done) if i_done is not None or r else None
                eng.tensor_tensor(ro[:, :], rank[:, i, r * NN:(r + 1) * NN], off[:, r, :], ALU.add).then_inc(S("ro"), 1)
                eng.wait_ge(S("ro"), N * r + i + 1)
                for j in range(TOPK):
                    eng.scalar_tensor_tensor(out=pjs[:, j, :], in0=col[:, :],
                                             scalar=recs[:, i, IDX + 4 * r + j:IDX + 4 * r + j + 1], in1=ro[:, :],
                                             op0=ALU.is_equal, op1=ALU.mult,
                                             accum_out=posf[:, j:j + 1]).then_inc(S("pj"), 1)
                eng.wait_ge(S("pj"), 4 * (N * r + i + 1))
                eng.tensor_copy(posI[:, r, u, :], posf[:, :]).then_inc(S(f"pos{r}"), 1)
                eng.tensor_copy(pos_all[:, i, r, :], posf[:, :]).then_inc(S("pall"), 1)

            def tick(t, u, has, first):
                if has(0):
                    if first >= 2:
                        eng.wait_ge(S(f"scat0{u}"), 64 * (t // 2) if isinstance(t, int) else (t - u) * 32)
                    positions(0, t, u, t if first >= 1 else None)

            ticks(eng, tick, 0)

            def expert(r):
                def tick(t, u, has, first):
                    if has(0):
                        eng.wait_ge(S(f"xTp{r}"), t + 1)
                        if first >= 2:
                            eng.wait_ge(S(f"prod{r}"), t - 1)
                        if r == 0:
                            eng.tensor_copy(xT[0:DH, u, 512:1024], psum[1][0:DH, :]).then_inc(S("xTV0"), 1)
                        else:
                            eng.tensor_copy(xT[:, u, 256:512], psum[1][:, 0:256]).then_inc(S("xTV1"), 1)
                    if has(1):
                        g = t - 1
                        eng.wait_ge(S(f"prod{r}"), g + 1)
                        if first >= 3:
                            eng.wait_ge(S(f"rows_out{r}{1 - u}"), (g // 2) * 16 if isinstance(g, int) else (g - 1 + u) * 8)
                        eng.tensor_copy(eo_of(r, 1 - u)[:, 2:4, :],
                                        psum[3 + 2 * (1 - u)][:, 0:2 * width_out[r]].rearrange("p (q d) -> p q d", q=2)
                                        ).then_inc(S(f"eoV{r}"), 1)

                ticks(eng, tick, 1, NG, G0)

            expert(0)
            for u in range(2):
                eng.wait_ge(S(f"scat0{u}"), 64 * ((N + 1 - u) // 2))
            eng.wait_ge(S("pall"), N)

            def tick(t, u, has, first):
                if has(0):
                    if first >= 2:
                        eng.wait_ge(S(f"gath{u}"), 64 * (t // 2) if isinstance(t, int) else (t - u) * 32)
                    eng.tensor_copy(gposI[:, u, :], pos_all[:, t, 0, :]).then_inc(S("gpos"), 1)
                    if first >= 2:
                        eng.wait_ge(S(f"scat1{u}"), 64 * (t // 2) if isinstance(t, int) else (t - u) * 32)
                    positions(1, t, u, t)
                if has(1):
                    i, v = t - 1, 1 - u
                    eng.wait_ge(S(f"gath{v}"), 64 * (i // 2) + 64 if isinstance(i, int) else (i - v) * 32 + 64)
                    for j in range(TOPK):
                        w = wts[:, i, 0, j:j + 1]
                        if j == 0:
                            eng.tensor_scalar(acc[:, 0, 0:R], got[:, v, 0, 0:R], w, None, ALU.mult).then_inc(S("mix"), 1)
                        else:
                            eng.wait_ge(S("mix"), 4 * i + j)
                            dst = rows_out[:, v, 0:R] if j == TOPK - 1 else acc[:, j, 0:R]
                            eng.scalar_tensor_tensor(out=dst, in0=got[:, v, j, 0:R], scalar=w, in1=acc[:, j - 1, 0:R],
                                                     op0=ALU.mult, op1=ALU.add).then_inc(S("mix"), 1)

            ticks(eng, tick, 1)
            expert(1)
            for u in range(2):
                eng.wait_ge(S(f"scat1{u}"), 64 * ((N + 1 - u) // 2))
            eng.wait_ge(S("pall"), 2 * N)

            def tick(t, u, has, first):
                if has(0):
                    if first >= 2:
                        eng.wait_ge(S(f"gathy{u}"), 64 * (t // 2) if isinstance(t, int) else (t - u) * 32)
                    eng.tensor_copy(gposI[:, u, :], pos_all[:, t, 1, :]).then_inc(S("gpos"), 1)
                if has(1):
                    i, v = t - 1, 1 - u
                    eng.wait_ge(S(f"gathy{v}"), 64 * (i // 2) + 64 if isinstance(i, int) else (i - v) * 32 + 64)
                    if first >= 3:
                        eng.wait_ge(S(f"out{v}"), 16 * (i // 2) if isinstance(i, int) else (i - v) * 8)
                    eng.wait_ge(S(f"resid{v}"), 16 * (i // 2) + 16 if isinstance(i, int) else (i - v) * 8 + 16)
                    for j in range(TOPK):
                        if j or first >= 2:
                            eng.wait_ge(S("ymix"), 4 * i + j)
                        dst = rows_out[:, v, :] if j == TOPK - 1 else acc[:, j, :]
                        src = resid[:, v, :] if j == 0 else acc[:, j - 1, :]
                        ins = eng.scalar_tensor_tensor(out=dst, in0=got[:, v, j, :], scalar=wts[:, i, 1, j:j + 1],
                                                       in1=src, op0=ALU.mult, op1=ALU.add)
                        ins.then_inc(S("ymix"), 1)
                    eng.wait_ge(S("ymix"), 4 * i + 4)
                    eng.sem_inc(S("y"), 1)

            ticks(eng, tick, 1)

        @block.tensor
        def _(eng):
            eng.wait_ge(S("einv"), 4)
            for r in range(2):
                last = eng.transpose(psum[4][:, r * NN:(r + 1) * NN], emb[:, r, :], ident[:, :])
            last.then_inc(S("embTp"), 1)
            eng.wait_ge(S("embT"), 1)
            eng.wait_ge(S("ld2"), 96)

            def tick(t, u, has, first):
                def count(weights, start, name):
                    for j in range(TOPK):
                        last = eng.matmul(psum[0][:, 0:2 * NN], weights[:, :], oh[:, j, :, :],
                                          start=(start and j == 0), stop=False, skip_group_check=True)
                    last.then_inc(S(name), 1)

                if has(4):
                    eng.wait_ge(S("oh"), 8 * (t - 4) + 8)
                    count(before, first == 4, "rankp")
                if has(1):
                    i = t - 1
                    hold(eng, "xn2", i + 1, "pe")
                    if first >= 2:
                        hold(eng, "hT2", i, "pe")
                    for k in range(2):
                        last = eng.transpose(psum[2][0:DH, k * 128:(k + 1) * 128], xn2[:, k * DH:(k + 1) * DH], ident[:, :])
                    last.then_inc(S("T3"), 1)
                if has(2):
                    i = t - 2
                    eng.wait_ge(S("qT"), i + 1)
                    if first >= 3:
                        eng.wait_ge(S("lg"), i)
                    eng.matmul(psum[1][:, 0:2 * NN], qT[:, :], embT[:, :, :], start=True, stop=True).then_inc(S("lgp"), 1)
                if has(4):
                    eng.wait_ge(S("rank"), t - 4 + 1)
                    count(upto, False, "ranku")
                if has(1):
                    i = t - 1
                    eng.wait_ge(S("hT2"), i + 1)
                    if first >= 2:
                        eng.wait_ge(S("qT"), i)
                    for k in range(2):
                        last = eng.matmul(psum[3][:, 0:128], wcat[:, k, :], hT2[:, k, :], start=(k == 0), stop=(k == 1))
                    last.then_inc(S("qp"), 1)

            ticks(eng, tick, 4)
            eng.wait_ge(S("ord"), 11)
            for r in range(2):
                for hh in range(2):
                    at = r * NT4 + hh * HT
                    last = eng.matmul(psum[1][0:1, at:at + HT], eidc[0:HT, r, hh:hh + 1], ident[0:HT, 0:HT],
                                      start=True, stop=True)
            last.then_inc(S("eidp"), 1)
            eng.wait_ge(S("ordered"), 1)

            for r in range(2):
                if r == 0:
                    eng.wait_ge(S("know2"), 32)
                else:
                    eng.wait_ge(S("rknow"), 64)
                kd = DH if r == 0 else 128
                nk = 2 if r == 0 else 1
                wo = width_out[r]
                regs = [eng.alloc_register(f"neuron{r}{q}") for q in range(GQ)]

                def tick(t, u, has, first, r=r, kd=kd, nk=nk, wo=wo, regs=regs):
                    if has(0):
                        hold(eng, f"rows_in{r}{u}", 16 * (t // 2) + 16 if isinstance(t, int) else (t - u) * 8 + 16, "pe")
                        if first >= 1:
                            hold(eng, f"xTA{r}", t, "pe")
                            hold(eng, f"xTV{r}", t, "pe")
                        for q in range(GQ):
                            for k in range(nk):
                                at = (q % 2) * nk * 128 + k * 128
                                last = eng.transpose(psum[q // 2][0:kd, at:at + 128],
                                                     xg_of(r, u)[:, q, k * kd:(k + 1) * kd], ident[:, :])
                        last.then_inc(S(f"xTp{r}"), 1)
                    if has(1):
                        g, v = t - 1, 1 - u
                        eng.load(regs, eid[0:1, r, bass.ds(g * GQ, GQ)])
                        vals = [eng.snap(x, min_val=0, max_val=NN - 1) for x in regs]
                        for who in "AV":
                            eng.wait_ge(S(f"xT{who}{r}"), g + 1)
                            if first >= 3:
                                eng.wait_ge(S(f"eo{who}{r}"), g - 1)
                        for q in range(GQ):
                            for k in range(nk):
                                at = (q * nk + k) * 128
                                last = eng.matmul(psum[2 + 2 * v + q // 2][:, (q % 2) * wo:(q % 2 + 1) * wo],
                                                  xT[0:kd, v, at:at + 128],
                                                  know[0:kd, bass.ds(vals[q] * (nk * wo) + k * wo, wo)],
                                                  start=(k == 0), stop=(k == nk - 1))
                        last.then_inc(S(f"prod{r}"), 1)

                ticks(eng, tick, 1, NG, G0)


_INS = ["x", "cls_tok", "L0_tok_W", "L0_tok_b", "L0_tok_gamma", "L0_tok_beta", "L0_attn_Wq", "L0_attn_Wk",
        "L0_attn_Wv", "L0_attn_Wgk1", "L0_attn_Wgk2", "L0_attn_bgk2", "L0_attn_Wg", "L0_attn_o_norm_w",
        "L0_attn_Wo", "L0_ffn_f_know", "L0_ffn_r_know", "L0_ffn_W_fk", "L0_ffn_b_fk", "L0_ffn_W_rk",
        "L0_ffn_b_rk", "L0_ffn_emb_fk", "L0_ffn_emb_rk"]
_OUTS = [((B, T, D), "float32")]


def kernel(**inputs):
    import numpy as _np
    import concourse.bacc as _bacc
    from concourse import mybir as _mybir
    from concourse.bass_utils import run_bass_kernel_spmd as _run

    nc = _bacc.Bacc("TRN2", target_bir_lowering=False, num_devices=1)
    arrays, args = {}, []
    for name in _INS:
        a = _np.ascontiguousarray(inputs[name])
        arrays[f"in_{name}_dram"] = a
        args.append(nc.dram_tensor(f"in_{name}_dram", a.shape, _mybir.dt.from_np(a.dtype), kind="ExternalInput").ap())
    for i, (shape, dtype) in enumerate(_OUTS):
        dt = _mybir.dt.from_np(_np.dtype(dtype))
        args.append(nc.dram_tensor(f"out_{i}_dram", shape, dt, kind="ExternalOutput").ap())
    vit_kernel(nc, *args)
    r = _run(nc, [arrays], core_ids=[0])
    got = tuple(r.results[0][f"out_{i}_dram"] for i in range(len(_OUTS)))
    return got[0]
```
